# Optimizing a Trainium2 kernel written in Bass

```python
import numpy as np
import jax
import jax.numpy as jnp

def _softmax(x, axis=-1):
    return jax.nn.softmax(x, axis=axis)

def _gelu(x):
    return jax.nn.gelu(x, approximate=True)

def _silu(x):
    return jax.nn.silu(x)

def _sigmoid(x):
    return jax.nn.sigmoid(x)

def _layernorm(x, axis=-1, eps=1e-05):
    m = jnp.mean(x, axis=axis, keepdims=True)
    v = jnp.var(x, axis=axis, keepdims=True)
    return (x - m) / jnp.sqrt(v + eps)

def _scatter_add(tgt, idx, src, axis=0):
    return tgt.at[idx].add(src)

def _segment_sum(src, seg, n):
    return jax.ops.segment_sum(src, seg, n)
kernel_name = 'mk_xattn_ffn_d1_seqx_r4_f8a158'

def setup_inputs(seed: int=0):
    np.random.seed(seed)
    _w = jnp.asarray

    def _rec_inputs():
        import jax
        import jax.numpy as jnp
        _rk = jax.random.key(seed)
        x = -0.000125 + 0.9999 * jax.random.normal(jax.random.fold_in(_rk, 1), (16, 112, 512), jnp.float32)
        _lenS = 112 - jax.random.randint(jax.random.fold_in(_rk, 7), (16,), 0, max(1, 112 // 4) + 1, jnp.int32)
        _lenS2 = 375 - jax.random.randint(jax.random.fold_in(_rk, 8), (16,), 0, max(1, 375 // 4) + 1, jnp.int32)
        _ctx_2048P = jax.random.normal(jax.random.fold_in(_rk, 11), (16, 16, 512), jnp.float32)
        _ctx_2048c = jax.random.dirichlet(jax.random.fold_in(_rk, 511), 0.3 * jnp.ones((16,), jnp.float32), (16, 375))
        _ctx_2048t = jnp.einsum('bsk,bkd->bsd', _ctx_2048c, _ctx_2048P)
        _ctx_2048t = _ctx_2048t * jax.lax.rsqrt(jnp.mean(jnp.square(_ctx_2048t)) + 1e-12) * 0.953939
        ctx_2048 = -0.000514642 + 1.00011 * (_ctx_2048t + 0.3 * jax.random.normal(jax.random.fold_in(_rk, 611), (16, 375, 512), jnp.float32))
        _validS = jnp.arange(112)[None, :] < _lenS[:, None]
        _validS2 = jnp.arange(375)[None, :] < _lenS2[:, None]
        _causal = jnp.tril(jnp.ones((112, 112), dtype=bool))
        mask_BxS2_bk0 = jnp.logical_not(jnp.broadcast_to(_validS2[:, :], (16, 375)))
        return (x, ctx_2048, mask_BxS2_bk0)
    x, ctx_2048, mask_BxS2_bk0 = _rec_inputs()

    def _L0_xattn_setup():
        import jax, jax.numpy as jnp
        import numpy as np
        key = jax.random.key(seed)
        k1, k2, k3 = jax.random.split(key, 3)
        B, S, D, M = (8, 512, 512, 128)
        hidden_states = jax.random.normal(k1, (B, S, D), dtype=jnp.float32)
        memory_tokens = jax.random.normal(k2, (B, M, D), dtype=jnp.float32)
        memory_mask = jax.random.randint(k3, (B, M), 0, 2).astype(jnp.bool_)
        return {'hidden_states': hidden_states, 'memory_tokens': memory_tokens, 'memory_mask': memory_mask}
    _L0_xattn_all = _L0_xattn_setup()
    _L0_xattn_in = {k: v for k, v in _L0_xattn_all.items() if k in ()}
    del _L0_xattn_all

    def _L0_ffn_setup():
        import jax, jax.numpy as jnp
        import numpy as np
        from jax import lax
        E = 64
        TOP_K = 8
        SEL_K = 4
        THRESH = 0.5
        H = 512
        F_INT = 192
        B, S = (1, 512)
        key = jax.random.key(seed)
        k0, k1, k2, k3, k4 = jax.random.split(key, 5)
        return {'hidden_states': jax.random.normal(k0, (B, S, H), jnp.float32), 'gate_weight': jax.random.normal(k1, (E, H), jnp.float32) * 0.02, 'gate_up_proj': jax.random.normal(k2, (E, 2 * F_INT, H), jnp.float32) * 0.02, 'down_proj': jax.random.normal(k3, (E, H, F_INT), jnp.float32) * 0.02, 'similarity': jax.random.uniform(k4, (E, E), jnp.float32)}
    _L0_ffn_all = _L0_ffn_setup()
    _L0_ffn_in = {k: v for k, v in _L0_ffn_all.items() if k in ('gate_weight', 'gate_up_proj', 'down_proj', 'similarity')}
    del _L0_ffn_all
    return {'x': x, 'ctx_2048': ctx_2048, 'mask_BxS2_bk0': mask_BxS2_bk0, 'L0_ffn_gate_weight': _L0_ffn_in['gate_weight'], 'L0_ffn_gate_up_proj': _L0_ffn_in['gate_up_proj'], 'L0_ffn_down_proj': _L0_ffn_in['down_proj'], 'L0_ffn_similarity': _L0_ffn_in['similarity']}

def reference(x, ctx_2048, mask_BxS2_bk0, L0_ffn_gate_weight, L0_ffn_gate_up_proj, L0_ffn_down_proj, L0_ffn_similarity):
    import jax
    import jax.numpy as jnp

    def _L0_xattn_ref(hidden_states, memory_tokens, memory_mask):
        import jax, jax.numpy as jnp
        import numpy as np
        B, S, D = hidden_states.shape
        scale = 1.0 / jnp.sqrt(jnp.asarray(D, hidden_states.dtype))
        scores = jnp.einsum('bsd,bmd->bsm', hidden_states, memory_tokens) * scale
        neg_inf = jnp.asarray(-1e+30, scores.dtype)
        scores = jnp.where(memory_mask[:, None, :], scores, neg_inf)
        attn = jax.nn.softmax(scores, axis=-1)
        readout = jnp.einsum('bsm,bmd->bsd', attn, memory_tokens)
        valid_b = jnp.any(memory_mask, axis=-1)
        out = jnp.where(valid_b[:, None, None], readout, jnp.zeros_like(readout))
        return out

    def _L0_ffn_ref(hidden_states, gate_weight, gate_up_proj, down_proj, similarity):
        import jax, jax.numpy as jnp
        import numpy as np
        from jax import lax
        E = 64
        TOP_K = 8
        SEL_K = 4
        THRESH = 0.5
        H = 512
        F_INT = 192
        B, S = (1, 512)
        b, s, h = hidden_states.shape
        x = hidden_states.reshape(-1, h)
        logits = x @ gate_weight.T
        probs = jax.nn.softmax(logits.astype(jnp.float32), axis=-1).astype(logits.dtype)
        top_val, top_idx = lax.top_k(probs, TOP_K)
        top_val = top_val / jnp.clip(top_val.sum(-1, keepdims=True), 1e-12)
        sim = similarity.astype(jnp.float32)
        diag = jnp.arange(E)
        sim = sim.at[diag, diag].set(1.0)
        primary_mask = jnp.zeros((E,), bool).at[top_idx[:, :SEL_K].reshape(-1)].set(True)
        secondary_mask = jnp.zeros((E,), bool).at[top_idx[:, SEL_K:].reshape(-1)].set(True)
        cand = jnp.where(primary_mask[None, :], sim, -jnp.inf)
        best_primary = jnp.argmax(cand, axis=-1)
        best_sim = jnp.max(cand, axis=-1)
        replace = secondary_mask & ~primary_mask & (best_sim >= THRESH)
        mapping = jnp.where(replace, best_primary, jnp.arange(E))
        rerouted = mapping[top_idx]
        rerouted = rerouted.at[:, :SEL_K].set(top_idx[:, :SEL_K])
        flat_e = rerouted.reshape(-1)
        order = jnp.argsort(flat_e)
        tok = order // TOP_K
        xs = x[tok]
        group_sizes = jnp.zeros((E,), jnp.int32).at[flat_e].add(1)
        gu = lax.ragged_dot(xs, jnp.swapaxes(gate_up_proj, 1, 2), group_sizes)
        gate, up = jnp.split(gu, 2, axis=-1)
        hact = jax.nn.silu(gate) * up
        y = lax.ragged_dot(hact, jnp.swapaxes(down_proj, 1, 2), group_sizes)
        w = top_val.reshape(-1)[order]
        out = jnp.zeros_like(x).at[tok].add(y * w[:, None])
        return out.reshape(b, s, h)
    x = x + _L0_xattn_ref(_layernorm(x, axis=-1), ctx_2048, mask_BxS2_bk0)
    x = x + _L0_ffn_ref(_layernorm(x, axis=-1), L0_ffn_gate_weight, L0_ffn_gate_up_proj, L0_ffn_down_proj, L0_ffn_similarity)
    return x

_drawn_inputs = setup_inputs


def setup_inputs(seed=0):
    import zlib

    import numpy as np

    out = dict(_drawn_inputs(seed))
    spreads = {}
    factors = {'L0_ffn_gate_weight': 6.136, 'L0_ffn_gate_up_proj': 5.499, 'L0_ffn_down_proj': 5.502}
    for name, (base, spread) in spreads.items():
        noise = np.random.default_rng([zlib.crc32(name.encode()), seed]).standard_normal(out[name].shape)
        drawn = base * np.exp(spread * noise) if base else spread * noise
        out[name] = jnp.asarray(drawn.astype(out[name].dtype))
    for name, factor in factors.items():
        out[name] = (out[name] * factor).astype(out[name].dtype)
    return out
```

```python
from contextlib import ExitStack

import concourse.bass as bass
from concourse import mybir

ALU = mybir.AluOpType
ACT = mybir.ActivationFunctionType
AX = mybir.AxisListType.X
F32 = mybir.dt.float32
F32R = mybir.dt.float32r
BF16 = mybir.dt.bfloat16
I32 = mybir.dt.int32
U32 = mybir.dt.uint32
U8 = mybir.dt.uint8

P = 128
B, T, D = 16, 112, 512
M, MC = 375, 125
MK = M // MC
DK = D // P
E, TOPK, SELK = 64, 8, 4
THRESH = 0.5
F = 192
FR = F - P
TOK = B * T
LIST = TOK
UNIT = 256
OVER = 128
PAD_LIST = E * LIST
ROWS = TOK + UNIT
MAX_OVER = 128
EPS = 1e-5
SCALE = float(D) ** -0.5
NEG = 1e30
LOW_KEY = -87.33


class At:

    def __init__(self, g, off, kind=None):
        self.g, self.off, self.kind = g, off, kind
        self.par = off % 2
        self.turn = g + off // 2 if not isinstance(g, int) or g else off // 2
        self.n = g * 2 + off if not isinstance(g, int) or g else off

    def __sub__(self, lag):
        return At(self.g, self.off - lag, self.kind)


def program(nc, x, ctx, ctxT, mask, gwT, w1, w2a, w2b, sim, out):
    table = nc.dram_tensor("list_table", (PAD_LIST + UNIT, 2), F32, kind="Internal").ap()
    normed = nc.dram_tensor("normed_tokens", (ROWS, D), F32, kind="Internal").ap()
    plan_d = nc.dram_tensor("plan_rows", (MAX_OVER, 4), I32, kind="Internal").ap()

    with ExitStack() as stack:
        def sb(name, shape, dt=F32):
            return stack.enter_context(nc.sbuf_tensor(name, shape, dt))

        def two(name, shape, dt=F32):
            return [sb(f"{name}{i}", shape, dt) for i in range(2)]

        def rstd_tiles(name):
            return {k: sb(f"rstd_{name}_{k}", [T, 1]) for k in ("var", "log", "rough", "square", "half", "exact")}

        def sem(name):
            return stack.enter_context(nc.semaphore(name))

        def sem2(name):
            return [sem(f"{name}{i}") for i in range(2)]

        bank = [stack.enter_context(nc.psum_tensor(f"bank{i}", [P, 512], F32)) for i in range(8)]

        ident = sb("ident", [P, P])
        not_ident = sb("not_ident", [E, E])
        tri = sb("tri", [T, T], BF16)
        tri_incl = sb("tri_incl", [E, E], BF16)
        ident_b = sb("ident_b", [E, E], BF16)
        ones_b = sb("ones_b", [P, P], BF16)
        ones_f = sb("ones_f", [E, P])
        col_i = sb("col_i", [P, E], I32)
        col = sb("col", [P, E])
        list_base = sb("list_base", [P, E])
        thr_i = sb("thr_i", [P, E], I32)
        over_thr = sb("over_thr", [P, 12])
        pair_thr = sb("pair_thr", [P, E])
        row_i = sb("row_i", [P, 1], I32)
        row = sb("row", [P, 1])
        zeros = sb("zeros", [P, D])
        blank = sb("blank", [E, LIST // UNIT, UNIT, 2])
        sim_s = sb("sim_s", [E, E])
        gw_s = sb("gw_s", [P, DK, E])

        xa = two("x_for_norm", [T, D])
        xr = two("x_for_residual", [T, D])
        ctxT_s = two("ctxT_s", [P, DK, M])
        ctx_s = two("ctx_s", [MC, MK, D])
        mask_s = two("mask_s", [T, M], U8)
        st_a = sb("st_a", [T, 6]); mv_a = sb("mv_a", [T, 2]); rstd_a = rstd_tiles("a")
        xn = two("xn", [T, D])
        xnT = two("xnT", [P, DK, T])
        madd = sb("madd", [T, M])
        sc = two("scores", [T, M])
        nmax = two("nmax", [T, 1])
        pr = two("probs", [T, M])
        rsum = two("rsum", [T, 1])
        pT = two("probsT", [MC, MK, T])
        rinv = sb("rinv", [T, 1]); rval = sb("rval", [T, 1])
        st_c = sb("st_c", [T, 6]); mv_c = sb("mv_c", [T, 2]); rstd_c = rstd_tiles("c")
        x1 = two("x1", [T, D])
        xn2 = two("xn2", [T, D])
        xn2T = two("xn2T", [P, DK, T])
        lmax = sb("lmax", [T, 1])
        key = two("key", [T, E])
        key8 = two("key8", [T, TOPK])
        idx8 = sb("idx8", [T, TOPK], U32)
        idx8f = sb("idx8f", [T, TOPK])
        chosen = two("chosen", [T, TOPK, E], BF16)
        mk = two("mk", [T, 2, E], BF16)
        run = two("run", [T, 2, E], BF16)
        eall = sb("eall", [T, E])
        esum = two("esum", [T, 1])
        e8 = two("e8", [T, TOPK])
        einv = sb("einv", [T, 1]); p8 = sb("p8", [T, TOPK]); s8 = sb("s8", [T, 1])
        s8c = sb("s8c", [T, 1]); s8i = sb("s8i", [T, 1])
        place = sb("place", [T, E])
        placed = sb("placed", [T, TOPK, E])
        slot8f = sb("slot8f", [T, TOPK])
        slot8 = two("slot8", [T, TOPK], I32)
        entry = two("entry", [T, TOPK, 2])

        prim = sb("prim", [E, E]); pen = sb("pen", [E, E]); simd = sb("simd", [E, E])
        sime = sb("sime", [E, E]); cand = sb("cand", [E, E]); candm = sb("candm", [E, E])
        best = sb("best", [E, 8]); bidx = sb("bidx", [E, 8], U32); bidxf = sb("bidxf", [E, 1])
        cp = sb("cp", [E, 1]); tot = sb("tot", [E, 1]); sec = sb("sec", [E, 1])
        rep = sb("rep", [E, 1]); repl = sb("repl", [E, 1]); diff = sb("diff", [E, 1])
        mapping = sb("mapping", [E, 1])
        over_is = sb("over_is", [E, 12]); nover = sb("nover", [E, 1])
        nover_b = sb("nover_b", [E, P], BF16); map_b = sb("map_b", [E, P], BF16)
        cum = sb("cum", [P, E]); le = sb("le", [P, E]); len_ = sb("len_", [P, E])
        eid = sb("eid", [P, 1]); pre = sb("pre", [P, 1])
        ohm = sb("ohm", [P, E]); ohs = sb("ohs", [P, E])
        rel = sb("rel", [P, 1]); relv = sb("relv", [P, 1]); real = sb("real", [P, 1])
        pairs_is = sb("pairs_is", [P, E])
        planf = sb("planf", [P, 4])
        plani = sb("plani", [P, 4], I32)
        prow = sb("prow", [1, MAX_OVER * 4], I32)

        raw1 = two("raw1_", [P, DK * 2 * F])
        raw2 = two("raw2_", [P, 2, D])
        w1h = two("w1h", [P, DK, 2 * F], F32R)
        w1l = two("w1l", [P, DK, 2 * F], F32R)
        w2h = two("w2h", [P, 2, D], F32R)
        w2l = two("w2l", [P, D], F32R)
        lg = two("list_for_gather", [P, 2, 2])
        ls = two("list_for_scatter", [P, 2, 2])
        xg = two("xg", [P, 2, D])
        xh = two("xh", [P, DK, UNIT], F32R)
        xl = two("xl", [P, DK, UNIT], F32R)
        sg = sb("sg", [P, 2, UNIT])
        h = sb("h", [P, 2, UNIT])
        hh = two("hh", [P, 2, UNIT], F32R)
        hl = two("hl", [P, 2, UNIT], F32R)
        ys = two("ys", [P, 2, D])

        const_pool = sem("const_pool"); const_dve = sem("const_dve"); const_in = sem("const_in")
        filled = sem("filled")
        x_in = sem2("x_in"); xr_in = sem2("xr_in"); ctxT_in = sem2("ctxT_in"); ctx_in = sem2("ctx_in")
        mask_in = sem2("mask_in")
        x1_out = sem2("x1_out"); xn2_out = sem2("xn2_out")
        c_norm = sem("c_norm"); c_normed = sem("c_normed"); c_renorm = sem("c_renorm"); c_score = sem("c_score"); c_resid = sem("c_resid")
        c_top = sem("c_top"); c_place = sem("c_place")
        xnT_ps = sem("xnT_ps"); score_ps = sem("score_ps"); pT_ps = sem("pT_ps"); read_ps = sem("read_ps")
        xn2T_ps = sem("xn2T_ps"); logit_ps = sem("logit_ps"); place_ps = sem("place_ps")
        xnT_sb = sem("xnT_sb"); probs_sb = sem("probs_sb"); pT_sb = sem("pT_sb"); xn2T_sb = sem("xn2T_sb")
        exps_sb = sem("exps_sb"); rough_a = sem("rough_a"); rough_c = sem("rough_c")
        tabled = sem2("tabled")
        plan_ps = sem("plan_ps"); c_plan = sem("c_plan"); plan_out = sem("plan_out"); plan_in = sem("plan_in")
        w1_in = sem2("w1_in"); w2_in = sem2("w2_in"); lg_in = sem2("lg_in"); ls_in = sem2("ls_in")
        gathered = sem2("gathered"); scattered = sem("scattered")
        w1h_s = sem("w1h_s"); w1l_s = sem("w1l_s"); w2h_s = sem("w2h_s"); w2l_s = sem("w2l_s")
        xT_ps = sem("xT_ps"); gu_ps = sem("gu_ps"); y_ps = sem("y_ps")
        xh_s = sem("xh_s"); xl_s = sem("xl_s"); silu_s = sem("silu_s"); h_s = sem("h_s")
        hh_s = sem("hh_s"); hl_s = sem("hl_s"); ys_s = sem("ys_s")
        cleared = sem("cleared"); spacer = sem("spacer")

        NORM, NORMED, SCORE, RESID, RENORM, TOP, PLACE = 3, 4, 3, 6, 4, 8, 9

        def split_wait(eng, s, value):
            wait(eng, s, value)
            if not isinstance(value, int):
                eng.sem_inc(spacer, 1)

        def wait(eng, s, value):
            if not isinstance(value, int) or value > 0:
                eng.wait_ge(s, value)

        class Chain:
            def __init__(self, eng, s, links, n):
                self.eng, self.s, self.links, self.base, self.c = eng, s, links, n * links, 0

            def link(self, ins, alone=False):
                self.c += 1
                ins.then_inc(self.s, 1)
                if self.c < self.links:
                    (split_wait if alone else wait)(self.eng, self.s, self.base + self.c)

            def done(self):
                assert self.c == self.links, (self.c, self.links)

        def phase1(eng, body):
            for n in range(-2, 6):
                body(At(0, n))
            with eng.Fori(3, 7) as g:
                for j in range(2):
                    body(At(g, j))
            for n in range(14, 21):
                body(At(0, n))

        def batches(slot, *stages):
            for lag, stage in stages:
                b = slot - lag
                if not isinstance(b.g, int) or 0 <= b.off < B:
                    stage(b)

        def phase2(eng, pairs, body):
            for n in range(-3, 4):
                body(At(0, n))
            with eng.Fori(2, 30) as g:
                for j in range(2):
                    body(At(g, j, "main"))
            for n in range(60, 68):
                body(At(0, n))
            with eng.Fori(34, pairs + 32) as g:
                for j in range(2):
                    body(At(g, j, "over"))
            for j in range(2):
                body(At(pairs + 32, j, "last"))

        def units(slot, *stages):
            for lag, stage in stages:
                u = slot - lag
                if slot.kind == "last" and u.off >= 0:
                    continue
                if slot.kind is None:
                    if u.off < 0:
                        continue
                    u.kind = "main" if u.off < E else "over"
                if u.kind == "last":
                    u.kind = "over"
                stage(u)

        def tiles(u):
            return 2 if u.kind == "main" else 1

        def upto(u, back):
            if u.kind == "main" or (isinstance(u.g, int) and u.off - back < E):
                return (u.n - back + 1) * 2
            return u.n - back + 1 + E

        def before(u):
            return upto(u, 1)

        def before_par(u):
            return u.turn * 2 if u.kind == "main" else u.turn + E // 2

        def pairs_of(eng):
            eng.wait_ge(plan_in, 16)
            return eng.value_load(prow[0:1, 3:4], min_val=3, max_val=59)

        block = stack.enter_context(nc.Block())

        @block.sync
        def _(sp):
            sp.dma_start(gw_s[:], gwT).then_inc(const_in, 16)
            sp.dma_start(sim_s[:], sim).then_inc(const_in, 16)

            def load_early(b):
                split_wait(sp, c_normed, (b.n - 1) * NORMED)
                sp.dma_start(xa[b.par][:], x[bass.ds(b.n, 1)].rearrange("a t d -> (a t) d")).then_inc(x_in[b.par], 16)
                split_wait(sp, score_ps, b.n - 1)
                sp.dma_start(ctxT_s[b.par][:], ctxT[bass.ds(b.n, 1)].rearrange("a p c m -> (a p) c m")).then_inc(ctxT_in[b.par], 16)
                split_wait(sp, c_score, (b.n - 1) * SCORE)
                sp.dma_start(mask_s[b.par][:], mask[bass.ds(b.n, 1)].broadcast_to([T, M])).then_inc(mask_in[b.par], 16)

            def load_late(b):
                split_wait(sp, read_ps, b.n - 1)
                sp.dma_start(ctx_s[b.par][:], ctx[bass.ds(b.n, 1)].rearrange("a (c p) d -> (a p) c d", p=MC)).then_inc(ctx_in[b.par], 16)
                split_wait(sp, c_resid, (b.n - 1) * RESID)
                sp.dma_start(xr[b.par][:], x[bass.ds(b.n, 1)].rearrange("a t d -> (a t) d")).then_inc(xr_in[b.par], 16)

            def store(b):
                split_wait(sp, c_resid, b.n * RESID + 3)
                sp.dma_start(out[bass.ds(b.n * T, T), :], x1[b.par][:]).then_inc(x1_out[b.par], 16)

            def store_normed(b):
                split_wait(sp, c_renorm, (b.n + 1) * RENORM)
                sp.dma_start(normed[bass.ds(b.n * T, T), :], xn2[b.par][:]).then_inc(xn2_out[b.par], 16)

            def fill(b):
                sp.wait_ge(const_pool, 1)
                sp.dma_start(out[TOK:TOK + P, :], zeros[:]).then_inc(filled, 16)
                sp.dma_start(out[TOK + P:ROWS, :], zeros[:]).then_inc(filled, 16)
                sp.dma_start(normed[TOK:TOK + P, :], zeros[:]).then_inc(filled, 16)
                sp.dma_start(normed[TOK + P:ROWS, :], zeros[:]).then_inc(filled, 16)
                sp.wait_ge(const_pool, 2)
                sp.dma_start(table[0:PAD_LIST].rearrange("(e n) c -> e (n c)", e=E),
                             blank[:].rearrange("e a b c -> e (a b c)")).then_inc(filled, 16)
                sp.dma_start(table[PAD_LIST:PAD_LIST + UNIT].rearrange("(o n) c -> o (n c)", o=1),
                             blank[0:1, 0].rearrange("e b c -> e (b c)")).then_inc(filled, 16)

            def slot(s):
                batches(s, (-2, load_early), (-1, load_late))
                if isinstance(s.g, int) and s.off == -1:
                    fill(s)
                batches(s, (2, store_normed), (1, store))

            phase1(sp, slot)

            sp.wait_ge(c_plan, PLAN)
            sp.dma_start(plan_d, plani[:]).then_inc(plan_out, 16)
            sp.wait_ge(plan_out, 16)
            sp.dma_start(prow[:], plan_d.rearrange("(o r) c -> o (r c)", o=1)).then_inc(plan_in, 16)
            pairs = pairs_of(sp)
            for p in range(2):
                sp.wait_ge(tabled[p], B // 2 * TOPK * 16)

            def expert(u):
                if u.kind == "main":
                    return sp.value_load(prow[0:1, bass.ds(u.n * 4 + 2, 1)], min_val=0, max_val=E - 1)
                return sp.value_load(prow[0:1, bass.ds((u.n - E) * 4, 1)], min_val=0, max_val=E - 1)

            def first_entry(u):
                if u.kind == "main":
                    return u.n * LIST
                return sp.value_load(prow[0:1, bass.ds((u.n - E) * 4 + 1, 1)], min_val=0, max_val=PAD_LIST)

            def load_list(u, dst, s):
                n = tiles(u)
                rows = table[bass.ds(first_entry(u), n * P), :].rearrange("(t p) c -> p t c", p=P)
                sp.dma_start(dst[u.par][:, 0:n, :], rows).then_inc(s[u.par], 16)

            def load_w1(u):
                split_wait(sp, w1h_s, u.n - 1)
                split_wait(sp, w1l_s, u.n - 1)
                sp.dma_start(raw1[u.par][:], w1[bass.ds(expert(u), 1)].rearrange("a p f -> (a p) f")).then_inc(w1_in[u.par], 16)

            def load_w2(u):
                split_wait(sp, w2h_s, u.n - 1)
                split_wait(sp, w2l_s, u.n - 1)
                e = expert(u)
                sp.dma_start(raw2[u.par][:, 0, :], w2a[bass.ds(e, 1)].rearrange("a p f -> (a p) f")).then_inc(w2_in[u.par], 16)
                sp.dma_start(raw2[u.par][0:FR, 1, :], w2b[bass.ds(e, 1)].rearrange("a p f -> (a p) f")).then_inc(w2_in[u.par], 16)

            def load_for_gather(u):
                split_wait(sp, gathered[u.par], before_par(u) * 16)
                load_list(u, lg, lg_in)

            def load_for_scatter(u):
                split_wait(sp, scattered, upto(u, 2) * 16)
                load_list(u, ls, ls_in)

            def slot2(s):
                units(s, (-3, load_for_gather), (-2, load_w1), (-1, load_w2), (1, load_for_scatter))

            phase2(sp, pairs, slot2)
            n = pairs * 2 + E
            split_wait(sp, scattered, (pairs * 2 + 2 * E) * 16)
            for p in range(2):
                split_wait(sp, w1_in[p], (pairs + E // 2 + 1) * 16)
                split_wait(sp, gathered[p], (pairs + E // 2 + 1 + E // 2) * 16)
            split_wait(sp, w2_in[0], (pairs + E // 2 + 1) * 32)
            split_wait(sp, lg_in[0], (pairs + E // 2 + 2 - 1) * 16)
            split_wait(sp, lg_in[1], (pairs + E // 2 + 1) * 16)
            split_wait(sp, lg_in[0], (pairs + E // 2 + 2) * 16)

        @block.gpsimd
        def _(pool):
            nc.gpsimd.memset(zeros[:], 0.0).then_inc(const_pool, 1)
            nc.gpsimd.memset(blank[:], 0.0).then_inc(cleared, 1)
            pool.wait_ge(cleared, 1)
            nc.gpsimd.iota(blank[:].bitcast(I32)[:, :, :, 0], [[0, LIST // UNIT], [1, UNIT]], base=TOK,
                           channel_multiplier=0).then_inc(const_pool, 1)
            nc.gpsimd.memset(ident[:], 0.0).then_inc(cleared, 1)
            nc.gpsimd.memset(tri[:], 1.0).then_inc(cleared, 1)
            nc.gpsimd.memset(tri_incl[:], 1.0).then_inc(cleared, 1)
            nc.gpsimd.memset(ident_b[:], 0.0).then_inc(cleared, 1)
            pool.wait_ge(cleared, 5)
            nc.gpsimd.affine_select(out=ident[:], in_=ident[:], compare_op=ALU.not_equal, fill=1.0, base=0,
                                    pattern=[[-1, P]], channel_multiplier=1).then_inc(const_pool, 1)
            nc.gpsimd.affine_select(out=tri[:], in_=tri[:], compare_op=ALU.is_gt, fill=0.0, base=0,
                                    pattern=[[1, T]], channel_multiplier=-1).then_inc(const_pool, 1)
            nc.gpsimd.affine_select(out=tri_incl[:], in_=tri_incl[:], compare_op=ALU.is_ge, fill=0.0, base=0,
                                    pattern=[[1, E]], channel_multiplier=-1).then_inc(const_pool, 1)
            nc.gpsimd.affine_select(out=ident_b[:], in_=ident_b[:], compare_op=ALU.not_equal, fill=1.0, base=0,
                                    pattern=[[-1, E]], channel_multiplier=1).then_inc(const_pool, 1)
            nc.gpsimd.memset(ones_b[:], 1.0).then_inc(const_pool, 1)
            nc.gpsimd.memset(ones_f[:], 1.0).then_inc(const_pool, 1)
            nc.gpsimd.iota(col_i[:], [[1, E]], base=0, channel_multiplier=0).then_inc(const_pool, 1)
            nc.gpsimd.iota(row_i[:], [[0, 1]], base=0, channel_multiplier=1).then_inc(const_pool, 1)
            for p in range(2):
                nc.gpsimd.iota(entry[p][:].bitcast(I32)[:, :, 0], [[0, TOPK]], base=T * (p - 2),
                               channel_multiplier=1).then_inc(const_pool, 1)
            nc.gpsimd.memset(planf[:], 0.0).then_inc(const_pool, 1)
            nc.gpsimd.memset(run[0][:], 0.0).then_inc(const_pool, 1)
            nc.gpsimd.memset(sg[:], 0.0).then_inc(const_pool, 1)

            pool.wait_ge(filled, 6 * 16)

            def enter(b):
                split_wait(pool, c_place, (b.n + 1) * PLACE)
                for k in range(TOPK):
                    pool.indirect_dma_start(table, bass.IndirectOffsetOnAxis(ap=slot8[b.par][:, k:k + 1], axis=0),
                                            entry[b.par][:, k, :], None).then_inc(tabled[b.par], 16)

            phase1(pool, lambda s: batches(s, (4, enter)))

            pairs = pairs_of(pool)
            for p in range(2):
                pool.wait_ge(xn2_out[p], B // 2 * 16)
                pool.wait_ge(x1_out[p], B // 2 * 16)

            def gather(u):
                split_wait(pool, lg_in[u.par], (u.turn + 1) * 16)
                split_wait(pool, xT_ps, upto(u, 2))
                for t in range(tiles(u)):
                    pool.indirect_dma_start(xg[u.par][:, t, :], None, normed,
                                            bass.IndirectOffsetOnAxis(ap=lg[u.par][:].bitcast(I32)[:, t, 0:1], axis=0)
                                            ).then_inc(gathered[u.par], 16)

            def scatter(u):
                split_wait(pool, ys_s, before(u) + tiles(u))
                split_wait(pool, scattered, before(u) * 16)
                for t in range(tiles(u)):
                    pool.indirect_dma_start(out, bass.IndirectOffsetOnAxis(ap=ls[u.par][:].bitcast(I32)[:, t, 0:1], axis=0),
                                            ys[u.par][:, t, :], None, compute_op=ALU.add).then_inc(scattered, 16)

            phase2(pool, pairs, lambda s: units(s, (-2, gather), (2, scatter)))

        @block.vector
        def _(dve):
            v = nc.vector
            dve.wait_ge(const_pool, 15)
            v.tensor_copy(col[:], col_i[:]).then_inc(const_dve, 1)
            v.tensor_copy(row[:], row_i[:]).then_inc(const_dve, 1)
            v.tensor_scalar(not_ident[:], ident[0:E, 0:E], -1.0, 1.0, ALU.mult, ALU.add).then_inc(const_dve, 1)
            dve.wait_ge(const_dve, 3)
            v.tensor_scalar(list_base[:], col[:], float(LIST), None, ALU.mult).then_inc(const_dve, 1)
            v.tensor_scalar(over_thr[:], col[:, 0:12], float(OVER), float(UNIT), ALU.mult, ALU.add).then_inc(const_dve, 1)
            v.tensor_scalar(pair_thr[:], col[:], 2.0, 6.0, ALU.mult, ALU.add).then_inc(const_dve, 1)
            dve.wait_ge(const_dve, 6)

            def norm(b):
                ch = Chain(dve, c_norm, NORM, b.n)
                dve.wait_ge(x_in[b.par], (b.turn + 1) * 16)
                ch.link(v.bn_stats(st_a[:], xa[b.par][:]), alone=True)
                ch.link(v.bn_aggr(mv_a[:], st_a[:]))
                ch.link(v.tensor_scalar(rstd_a["var"][:], mv_a[:, 1:2], EPS, None, ALU.add))
                ch.done()

            def newton(ch, r):
                ch.link(v.tensor_tensor(r["square"][:], r["rough"][:], r["rough"][:], ALU.mult))
                ch.link(v.tensor_scalar(r["half"][:], r["square"][:], r["var"][:], -0.5, ALU.mult, ALU.mult))
                ch.link(v.scalar_tensor_tensor(r["exact"][:], r["half"][:], 1.5, r["rough"][:], ALU.add, ALU.mult))

            def normed_x(b):
                ch = Chain(dve, c_normed, NORMED, b.n)
                dve.wait_ge(rough_a, (b.n + 1) * 2)
                newton(ch, rstd_a)
                wait(dve, xnT_ps, b.n - 1)
                ch.link(v.tensor_scalar(xn[b.par][:], xa[b.par][:], mv_a[:, 0:1], rstd_a["exact"][:], ALU.subtract, ALU.mult))
                ch.done()

            def score(b):
                ch = Chain(dve, c_score, SCORE, b.n)
                dve.wait_ge(mask_in[b.par], (b.turn + 1) * 16)
                ch.link(v.tensor_scalar(madd[:], mask_s[b.par][:], -1.0, NEG, ALU.add, ALU.mult))
                dve.wait_ge(score_ps, b.n + 1)
                wait(dve, probs_sb, b.n - 1)
                wait(dve, c_resid, (b.n - 1) * RESID)
                ch.link(v.scalar_tensor_tensor(sc[b.par][:], bank[1][0:T, 0:M], SCALE, madd[:], ALU.mult, ALU.add))
                ch.link(v.tensor_reduce(nmax[b.par][:], sc[b.par][:], AX, ALU.max, negate=True))
                ch.done()

            def resid(b):
                ch = Chain(dve, c_resid, RESID, b.n)
                dve.wait_ge(probs_sb, b.n + 1)
                ch.link(v.reciprocal(rinv[:], rsum[b.par][:]))
                ch.link(v.tensor_scalar(rval[:], nmax[b.par][:], NEG / 2, rinv[:], ALU.is_lt, ALU.mult))
                dve.wait_ge(xr_in[b.par], (b.turn + 1) * 16)
                dve.wait_ge(read_ps, b.n + 1)
                wait(dve, x1_out[b.par], b.turn * 16)
                ch.link(v.scalar_tensor_tensor(x1[b.par][:], bank[3][0:T, :], rval[:], xr[b.par][:], ALU.mult, ALU.add))
                ch.link(v.bn_stats(st_c[:], x1[b.par][:]), alone=True)
                ch.link(v.bn_aggr(mv_c[:], st_c[:]))
                ch.link(v.tensor_scalar(rstd_c["var"][:], mv_c[:, 1:2], EPS, None, ALU.add))
                ch.done()

            def renormed_x(b):
                ch = Chain(dve, c_renorm, RENORM, b.n)
                dve.wait_ge(rough_c, (b.n + 1) * 2)
                newton(ch, rstd_c)
                wait(dve, xn2T_ps, b.n - 1)
                wait(dve, xn2_out[b.par], b.turn * 16)
                ch.link(v.tensor_scalar(xn2[b.par][:], x1[b.par][:], mv_c[:, 0:1], rstd_c["exact"][:], ALU.subtract, ALU.mult))
                ch.done()

            def top(b):
                ch = Chain(dve, c_top, TOP, b.n)
                dve.wait_ge(logit_ps, b.n + 1)
                ch.link(v.tensor_reduce(lmax[:], bank[5][0:T, 0:E], AX, ALU.max))
                wait(dve, exps_sb, b.n - 1)
                ch.link(v.tensor_scalar(key[b.par][:], bank[5][0:T, 0:E], lmax[:], LOW_KEY, ALU.subtract, ALU.max), alone=True)
                ch.link(v.max(key8[b.par][:], key[b.par][:]), alone=True)
                ch.link(v.max_index(idx8[:], key8[b.par][:], key[b.par][:]))
                ch.link(v.tensor_copy(idx8f[:], idx8[:]))
                ch.link(v.tensor_tensor(chosen[b.par][:], col[0:T].unsqueeze(1).to_broadcast([T, TOPK, E]),
                                        idx8f[:].unsqueeze(2).to_broadcast([T, TOPK, E]), ALU.is_equal))
                wait(dve, place_ps, b.n - 1)
                with nc.allow_low_precision(reason="each sum is 0 or 1"):
                    ch.link(v.tensor_reduce(mk[b.par][:], chosen[b.par][:].rearrange("t (s k) e -> t s e k", s=2), AX, ALU.add))
                ch.link(v.tensor_tensor(run[1 - b.par][:], run[b.par][:], mk[b.par][:], ALU.add))
                ch.done()

            def place_entries(b):
                ch = Chain(dve, c_place, PLACE, b.n)
                dve.wait_ge(exps_sb, b.n + 1)
                wait(dve, tabled[b.par], b.turn * TOPK * 16)
                ch.link(v.reciprocal(einv[:], esum[b.par][:]))
                ch.link(v.tensor_scalar(p8[:], e8[b.par][:], einv[:], None, ALU.mult))
                ch.link(v.tensor_reduce(s8[:], p8[:], AX, ALU.add))
                ch.link(v.tensor_scalar(s8c[:], s8[:], 1e-12, None, ALU.max))
                ch.link(v.reciprocal(s8i[:], s8c[:]))
                v.tensor_scalar(entry[b.par][:, :, 1], p8[:], s8i[:], None, ALU.mult)
                v.tensor_scalar(entry[b.par][:].bitcast(I32)[:, :, 0], entry[b.par][:].bitcast(I32)[:, :, 0],
                                2 * T, None, ALU.add)
                dve.wait_ge(place_ps, b.n + 1)
                ch.link(v.tensor_tensor(place[:], bank[6][0:T, 0:E], list_base[0:T, :], ALU.add))
                ch.link(v.tensor_tensor(placed[:], chosen[b.par][:], place[:].unsqueeze(1).to_broadcast([T, TOPK, E]), ALU.mult))
                ch.link(v.tensor_reduce(slot8f[:], placed[:], AX, ALU.add))
                ch.link(v.tensor_copy(slot8[b.par][:], slot8f[:]))
                ch.done()

            phase1(dve, lambda s: batches(s, (2, renormed_x), (4, place_entries), (3, top), (-1, norm), (0, score),
                                          (-1, normed_x), (1, resid)))

            ch = Chain(dve, c_plan, PLAN, 0)
            dve.wait_ge(const_in, 32)
            dve.wait_ge(plan_ps, 1)
            ch.link(v.tensor_scalar(prim[:], bank[7][0:E, 0:E], 0.0, None, ALU.is_gt))
            ch.link(v.tensor_copy(cp[:], bank[7][0:E, 64:65]))
            ch.link(v.tensor_copy(tot[:], bank[7][0:E, 80:81]))
            ch.link(v.tensor_tensor(simd[:], sim_s[:], not_ident[:], ALU.mult))
            ch.link(v.tensor_tensor(sime[:], simd[:], ident[0:E, 0:E], ALU.add))
            ch.link(v.tensor_tensor(candm[:], sime[:], prim[:], ALU.mult))
            ch.link(v.tensor_scalar(pen[:], prim[:], -1.0, NEG, ALU.add, ALU.mult))
            ch.link(v.tensor_tensor(cand[:], candm[:], pen[:], ALU.add))
            ch.link(v.max(best[:], cand[:]))
            ch.link(v.max_index(bidx[:], best[:], cand[:]))
            ch.link(v.tensor_copy(bidxf[:], bidx[:, 0:1]))
            ch.link(v.tensor_tensor(sec[:], tot[:], cp[:], ALU.is_gt))
            ch.link(v.tensor_scalar(rep[:], cp[:], 0.0, sec[:], ALU.is_le, ALU.mult))
            ch.link(v.tensor_scalar(repl[:], best[:, 0:1], THRESH, rep[:], ALU.is_ge, ALU.mult))
            ch.link(v.tensor_tensor(diff[:], bidxf[:], row[0:E], ALU.subtract))
            ch.link(v.scalar_tensor_tensor(mapping[:], diff[:], repl[:], row[0:E], ALU.mult, ALU.add))
            ch.link(v.tensor_scalar(over_is[:], over_thr[0:E, :], tot[:], None, ALU.is_lt))
            ch.link(v.tensor_reduce(nover[:], over_is[:], AX, ALU.add))
            ch.link(v.tensor_scalar(nover_b[:], ones_f[:], nover[:], None, ALU.mult))
            ch.link(v.tensor_scalar(map_b[:], ones_f[:], mapping[:], None, ALU.mult))
            assert ch.c == PLAN_A
            dve.wait_ge(plan_ps, 2)
            ch.link(v.tensor_scalar(le[:], bank[7][:, 128:192], row[:], None, ALU.is_le))
            ch.link(v.tensor_reduce(eid[:], le[:], AX, ALU.add))
            ch.link(v.tensor_tensor(len_[:], bank[7][:, 192:256], le[:], ALU.mult))
            ch.link(v.tensor_reduce(pre[:], len_[:], AX, ALU.add))
            ch.link(v.tensor_scalar(ohs[:], col[:], eid[:], None, ALU.is_equal))
            ch.link(v.tensor_tensor(ohm[:], bank[7][:, 256:320], ohs[:], ALU.mult))
            ch.link(v.tensor_reduce(planf[:, 0:1], ohm[:], AX, ALU.add))
            ch.link(v.tensor_tensor(rel[:], row[:], pre[:], ALU.subtract))
            ch.link(v.tensor_scalar(relv[:], rel[:], float(OVER), float(UNIT), ALU.mult, ALU.add))
            ch.link(v.tensor_scalar(real[:], eid[:], float(E), relv[:], ALU.is_lt, ALU.mult))
            ch.link(v.scalar_tensor_tensor(planf[:, 1:2], eid[:], float(LIST), real[:], ALU.mult, ALU.add))
            ch.link(v.tensor_copy(planf[0:E, 2:3], mapping[:]))
            ch.link(v.tensor_copy(cum[:], bank[7][:, 128:192]))
            ch.link(v.tensor_scalar(pairs_is[:], pair_thr[:], cum[:, E - 1:E], None, ALU.is_lt))
            ch.link(v.tensor_reduce(pre[:], pairs_is[:], AX, ALU.add))
            ch.link(v.tensor_scalar(planf[:, 3:4], pre[:], 3.0, None, ALU.add))
            ch.link(v.tensor_copy(plani[:], planf[:]))
            ch.done()

            pairs = pairs_of(dve)

            def h_products(u):
                W = tiles(u) * P
                dve.wait_ge(silu_s, (u.n + 1) * 2)
                dve.wait_ge(gu_ps, u.n + 1)
                wait(dve, hh_s, u.n)
                wait(dve, hl_s, u.n)
                ab, c = bank[u.par], bank[2 + u.par]
                v.tensor_tensor(h[:, 0, 0:W], sg[:, 0, 0:W], ab[:, UNIT:UNIT + W], ALU.mult).then_inc(h_s, 1)
                v.tensor_tensor(h[0:FR, 1, 0:W], sg[0:FR, 1, 0:W], c[FR:P, 0:W], ALU.mult).then_inc(h_s, 1)
                v.tensor_tensor(h[FR:P, 1, 0:W], sg[0:FR, 1, 0:W], c[FR:P, 0:W], ALU.mult).then_inc(h_s, 1)

            def h_low(u):
                W = tiles(u) * P
                dve.wait_ge(hh_s, u.n + 1)
                wait(dve, y_ps, upto(u, 2))
                v.tensor_tensor(hl[u.par][:, :, 0:W], h[:, :, 0:W], hh[u.par][:, :, 0:W].bitcast(F32),
                                ALU.subtract).then_inc(hl_s, 1)

            def x_low(u):
                wait(dve, gu_ps, u.n - 1)
                for t in range(tiles(u)):
                    dve.wait_ge(xh_s, before(u) + t + 1)
                    v.tensor_tensor(xl[u.par][:, :, t * P:(t + 1) * P], bank[6 + t][:].rearrange("p (c t) -> p c t", c=DK),
                                    xh[u.par][:, :, t * P:(t + 1) * P].bitcast(F32), ALU.subtract).then_inc(xl_s, 1)

            def w1_low(u):
                dve.wait_ge(w1h_s, u.n + 1)
                wait(dve, gu_ps, u.n - 1)
                v.tensor_tensor(w1l[u.par][:].rearrange("p c f -> p (c f)"), raw1[u.par][:],
                                w1h[u.par][:].rearrange("p c f -> p (c f)").bitcast(F32), ALU.subtract).then_inc(w1l_s, 1)

            def w2_low(u):
                dve.wait_ge(w2h_s, u.n + 1)
                wait(dve, y_ps, upto(u, 2))
                v.tensor_tensor(w2l[u.par][:], raw2[u.par][:, 0, :], w2h[u.par][:, 0, :].bitcast(F32), ALU.subtract)
                v.tensor_tensor(w2h[u.par][FR:P, 1, :], raw2[u.par][0:FR, 1, :], w2h[u.par][0:FR, 1, :].bitcast(F32),
                                ALU.subtract).then_inc(w2l_s, 1)

            phase2(dve, pairs, lambda s: units(s, (1, h_products), (-1, w1_low), (1, h_low), (-1, x_low), (0, w2_low)))

        @block.scalar
        def _(act):
            a = nc.scalar

            def copy_pT(b):
                act.wait_ge(pT_ps, b.n + 1)
                wait(act, read_ps, b.n - 1)
                a.copy(pT[b.par][:], bank[2][0:MC, 0:MK * T].rearrange("p (c t) -> p c t", c=MK)).then_inc(pT_sb, 1)

            def copy_xn2T(b):
                act.wait_ge(xn2T_ps, b.n + 1)
                wait(act, logit_ps, b.n - 1)
                a.copy(xn2T[b.par][:], bank[4][:, 0:DK * T].rearrange("p (c t) -> p c t", c=DK)).then_inc(xn2T_sb, 1)

            def exps(b):
                act.wait_ge(c_top, b.n * TOP + 3)
                wait(act, c_place, (b.n - 1) * PLACE)
                wait(act, exps_sb, b.n)
                a.activation(eall[:], key[b.par][:], ACT.Exp, accum_out=esum[b.par][:])
                a.activation(e8[b.par][:], key8[b.par][:], ACT.Exp).then_inc(exps_sb, 1)

            def exp_scores(b):
                act.wait_ge(c_score, (b.n + 1) * SCORE)
                wait(act, c_resid, (b.n - 1) * RESID)
                wait(act, pT_ps, b.n - 1)
                a.activation(pr[b.par][:], sc[b.par][:], ACT.Exp, bias=nmax[b.par][:],
                             accum_out=rsum[b.par][:]).then_inc(probs_sb, 1)

            def copy_xnT(b):
                act.wait_ge(xnT_ps, b.n + 1)
                wait(act, score_ps, b.n - 1)
                a.copy(xnT[b.par][:], bank[0][:, 0:DK * T].rearrange("p (c t) -> p c t", c=DK)).then_inc(xnT_sb, 1)

            def rough(s, c, links, r):
                def stage(b):
                    act.wait_ge(c, (b.n + 1) * links)
                    a.activation(r["log"][:], r["var"][:], ACT.Ln).then_inc(s, 1)
                    act.wait_ge(s, b.n * 2 + 1)
                    a.activation(r["rough"][:], r["log"][:], ACT.Exp, scale=-0.5).then_inc(s, 1)
                return stage

            nc.scalar.preload_act_table_set("natural_log_exp_and_others")
            phase1(act, lambda s: batches(s, (1, copy_pT), (-1, rough(rough_a, c_norm, NORM, rstd_a)), (2, copy_xn2T),
                                          (3, exps), (0, exp_scores), (-1, copy_xnT),
                                          (1, rough(rough_c, c_resid, RESID, rstd_c))))

            nc.scalar.preload_act_table(ACT.Silu)
            pairs = pairs_of(act)

            def silu(u):
                W = tiles(u) * P
                act.wait_ge(gu_ps, u.n + 1)
                wait(act, h_s, u.n * 3)
                a.activation(sg[:, 0, 0:W], bank[u.par][:, 0:W], ACT.Silu).then_inc(silu_s, 1)
                a.activation(sg[0:FR, 1, 0:W], bank[2 + u.par][0:FR, 0:W], ACT.Silu).then_inc(silu_s, 1)

            def h_high(u):
                W = tiles(u) * P
                act.wait_ge(h_s, (u.n + 1) * 3)
                wait(act, y_ps, upto(u, 2))
                a.copy(hh[u.par][:, :, 0:W], h[:, :, 0:W]).then_inc(hh_s, 1)

            def y_out(u):
                act.wait_ge(ls_in[u.par], (u.turn + 1) * 16)
                wait(act, scattered, upto(u, 2) * 16)
                for t in range(tiles(u)):
                    act.wait_ge(y_ps, before(u) + t + 1)
                    a.activation(ys[u.par][:, t, :], bank[4 + t][:], ACT.Copy, scale=ls[u.par][:, t, 1:2]).then_inc(ys_s, 1)

            def x_high(u):
                wait(act, gu_ps, u.n - 1)
                for t in range(tiles(u)):
                    act.wait_ge(xT_ps, before(u) + t + 1)
                    a.copy(xh[u.par][:, :, t * P:(t + 1) * P],
                           bank[6 + t][:].rearrange("p (c t) -> p c t", c=DK)).then_inc(xh_s, 1)

            def w1_high(u):
                act.wait_ge(w1_in[u.par], (u.turn + 1) * 16)
                wait(act, gu_ps, u.n - 1)
                a.copy(w1h[u.par][:].rearrange("p c f -> p (c f)"), raw1[u.par][:]).then_inc(w1h_s, 1)

            def w2_high(u):
                act.wait_ge(w2_in[u.par], (u.turn + 1) * 32)
                wait(act, y_ps, upto(u, 2))
                a.copy(w2h[u.par][:, 0, :], raw2[u.par][:, 0, :])
                a.copy(w2h[u.par][0:FR, 1, :], raw2[u.par][0:FR, 1, :]).then_inc(w2h_s, 1)

            phase2(act, pairs, lambda s: units(s, (1, silu), (-1, w1_high), (1, h_high), (2, y_out), (-1, x_high), (0, w2_high)))

        @block.tensor
        def _(pe):
            pe.wait_ge(const_pool, 15)
            pe.wait_ge(const_in, 32)

            def turn_probs(b):
                pe.wait_ge(probs_sb, b.n + 1)
                wait(pe, pT_sb, b.n)
                for c in range(MK):
                    mm = pe.transpose(bank[2][0:MC, c * T:(c + 1) * T], pr[b.par][:, c * MC:(c + 1) * MC], ident[0:T, 0:T])
                mm.then_inc(pT_ps, 1)

            def turn_xn2(b):
                pe.wait_ge(c_renorm, (b.n + 1) * RENORM)
                wait(pe, xn2T_sb, b.n)
                for c in range(DK):
                    mm = pe.transpose(bank[4][:, c * T:(c + 1) * T], xn2[b.par][:, c * P:(c + 1) * P], ident[0:T, 0:T])
                mm.then_inc(xn2T_ps, 1)

            def scores(b):
                pe.wait_ge(ctxT_in[b.par], (b.turn + 1) * 16)
                pe.wait_ge(xnT_sb, b.n + 1)
                wait(pe, c_score, b.n * SCORE)
                for c in range(DK):
                    mm = pe.matmul(bank[1][0:T, 0:M], xnT[b.par][:, c, :], ctxT_s[b.par][:, c, :],
                                   start=(c == 0), stop=(c == DK - 1))
                mm.then_inc(score_ps, 1)

            def readout(b):
                pe.wait_ge(ctx_in[b.par], (b.turn + 1) * 16)
                pe.wait_ge(pT_sb, b.n + 1)
                wait(pe, c_resid, b.n * RESID)
                for c in range(MK):
                    mm = pe.matmul(bank[3][0:T, :], pT[b.par][:, c, :], ctx_s[b.par][:, c, :],
                                   start=(c == 0), stop=(c == MK - 1))
                mm.then_inc(read_ps, 1)

            def logits(b):
                pe.wait_ge(xn2T_sb, b.n + 1)
                wait(pe, c_top, b.n * TOP)
                for c in range(DK):
                    mm = pe.matmul(bank[5][0:T, 0:E], xn2T[b.par][:, c, :], gw_s[:, c, :],
                                   start=(c == 0), stop=(c == DK - 1))
                mm.then_inc(logit_ps, 1)

            def places(b):
                pe.wait_ge(c_top, (b.n + 1) * TOP)
                wait(pe, c_place, b.n * PLACE)
                for s in range(2):
                    pe.matmul(bank[6][0:T, 0:E], tri[:], mk[b.par][:, s, :], start=(s == 0), stop=False)
                for s in range(2):
                    mm = pe.matmul(bank[6][0:T, 0:E], ones_b[0:T, 0:T], run[b.par][:, s, :], start=False, stop=(s == 1))
                mm.then_inc(place_ps, 1)

            def turn_xn(b):
                pe.wait_ge(c_normed, (b.n + 1) * NORMED)
                wait(pe, xnT_sb, b.n)
                for c in range(DK):
                    mm = pe.transpose(bank[0][:, c * T:(c + 1) * T], xn[b.par][:, c * P:(c + 1) * P], ident[0:T, 0:T])
                mm.then_inc(xnT_ps, 1)

            phase1(pe, lambda s: batches(s, (1, turn_probs), (2, turn_xn2), (0, scores), (1, readout),
                                         (2, logits), (3, places), (-1, turn_xn)))

            pe.wait_ge(c_top, B * TOP)
            pe.matmul(bank[7][0:E, 0:E], ones_b[0:T, 0:E], run[0][:, 0, :], start=True, stop=True)
            pe.matmul(bank[7][0:E, 64:80], run[0][:, 0, :], ones_b[0:T, 0:16], start=True, stop=True)
            pe.matmul(bank[7][0:E, 80:96], run[0][:, 0, :], ones_b[0:T, 0:16], start=True, stop=False)
            pe.matmul(bank[7][0:E, 80:96], run[0][:, 1, :], ones_b[0:T, 0:16], start=False, stop=True).then_inc(plan_ps, 1)
            pe.wait_ge(c_plan, PLAN_A)
            pe.matmul(bank[7][:, 128:192], nover_b[:], tri_incl[:], start=True, stop=True)
            pe.matmul(bank[7][:, 192:256], nover_b[:], ident_b[:], start=True, stop=True)
            pe.matmul(bank[7][:, 256:320], map_b[:], ident_b[:], start=True, stop=True).then_inc(plan_ps, 1)

            pairs = pairs_of(pe)

            def turn_rows(u):
                pe.wait_ge(gathered[u.par], (before_par(u) + tiles(u)) * 16)
                wait(pe, xh_s, before(u))
                wait(pe, xl_s, before(u))
                for t in range(tiles(u)):
                    for c in range(DK):
                        mm = pe.transpose(bank[6 + t][:, c * P:(c + 1) * P], xg[u.par][:, t, c * P:(c + 1) * P], ident[:])
                    mm.then_inc(xT_ps, 1)

            def gate_up(u):
                W = tiles(u) * P
                pe.wait_ge(w1l_s, u.n + 1)
                pe.wait_ge(xl_s, before(u) + tiles(u))
                wait(pe, h_s, (u.n - 1) * 3)
                for m in range(3):
                    o = (bank[u.par][:, m * UNIT:m * UNIT + W] if m < 2 else bank[2 + u.par][:, 0:W])
                    for c in range(DK):
                        wh, wl = w1h[u.par][:, c, m * P:(m + 1) * P], w1l[u.par][:, c, m * P:(m + 1) * P]
                        mh, ml = xh[u.par][:, c, 0:W], xl[u.par][:, c, 0:W]
                        pe.matmul(o, wh, mh, start=(c == 0), stop=False)
                        pe.matmul(o, wh, ml, start=False, stop=False)
                        mm = pe.matmul(o, wl, mh, start=False, stop=(c == DK - 1))
                mm.then_inc(gu_ps, 1)

            def down(u):
                pe.wait_ge(hl_s, u.n + 1)
                pe.wait_ge(w2l_s, u.n + 1)
                wait(pe, ys_s, before(u))
                for t in range(tiles(u)):
                    s = slice(t * P, (t + 1) * P)
                    o = bank[4 + t][:]
                    pe.matmul(o, hh[u.par][:, 0, s], w2h[u.par][:, 0, :], start=True, stop=False)
                    pe.matmul(o, hh[u.par][:, 0, s], w2l[u.par][:], start=False, stop=False)
                    pe.matmul(o, hl[u.par][:, 0, s], w2h[u.par][:, 0, :], start=False, stop=False)
                    pe.matmul(o, hh[u.par][:, 1, s], w2h[u.par][:, 1, :], start=False, stop=False)
                    pe.matmul(o, hl[u.par][0:FR, 1, s], w2h[u.par][0:FR, 1, :], start=False, stop=True).then_inc(y_ps, 1)

            phase2(pe, pairs, lambda s: units(s, (-1, turn_rows), (0, gate_up), (1, down)))


PLAN_A = 20
PLAN = PLAN_A + 17


def kernel(x, ctx_2048, mask_BxS2_bk0, L0_ffn_gate_weight, L0_ffn_gate_up_proj, L0_ffn_down_proj, L0_ffn_similarity):
    import numpy as np
    import concourse.bacc as bacc
    from concourse.bass_utils import run_bass_kernel_spmd

    ctx = np.asarray(ctx_2048)
    ctxT = ctx.transpose(0, 2, 1).reshape(B, DK, P, M).transpose(0, 2, 1, 3)
    gwT = np.asarray(L0_ffn_gate_weight).T.reshape(DK, P, E).transpose(1, 0, 2)
    gu = np.asarray(L0_ffn_gate_up_proj)
    gate, up = gu[:, :F], gu[:, F:]
    w1 = np.concatenate([gate[:, :P], up[:, :P], gate[:, P:], up[:, P:]], axis=1)
    w1 = w1.transpose(0, 2, 1).reshape(E, DK, P, 2 * F).transpose(0, 2, 1, 3).reshape(E, P, DK * 2 * F)
    w2 = np.asarray(L0_ffn_down_proj).transpose(0, 2, 1)
    data = {
        "in_x": np.asarray(x), "in_ctx": ctx, "in_ctxT": ctxT,
        "in_mask": np.asarray(mask_BxS2_bk0), "in_gwT": gwT, "in_w1": w1,
        "in_w2a": w2[:, :P], "in_w2b": w2[:, P:], "in_sim": np.asarray(L0_ffn_similarity),
    }
    data = {k: np.ascontiguousarray(a) for k, a in data.items()}
    nc = bacc.Bacc("TRN2", target_bir_lowering=False, num_devices=1)
    args = [nc.dram_tensor(k, a.shape, mybir.dt.from_np(a.dtype), kind="ExternalInput").ap() for k, a in data.items()]
    args.append(nc.dram_tensor("out_rows", (ROWS, D), F32, kind="ExternalOutput").ap())
    program(nc, *args)
    rows = run_bass_kernel_spmd(nc, [data], core_ids=[0]).results[0]["out_rows"]
    return rows[:TOK].reshape(B, T, D)
```

```python
from contextlib import ExitStack

import concourse.bass as bass
from concourse import mybir

ALU = mybir.AluOpType
ACT = mybir.ActivationFunctionType
AX = mybir.AxisListType.X
F32 = mybir.dt.float32
F32R = mybir.dt.float32r
BF16 = mybir.dt.bfloat16
I32 = mybir.dt.int32
U32 = mybir.dt.uint32
U8 = mybir.dt.uint8

P = 128
B, T, D = 16, 112, 512
M, MC = 375, 125
MK = M // MC
DK = D // P
E, TOPK, SELK = 64, 8, 4
THRESH = 0.5
F = 192
FR = F - P
TOK = B * T
LIST = TOK
UNIT = 256
OVER = 128
PAD_LIST = E * LIST
ROWS = TOK + UNIT
ROW = D + E
PCOLS = 5
NSENT = TOPK - SELK
MAX_OVER = 128
EPS = 1e-5
SCALE = float(D) ** -0.5
NEG = 1e30
LOW_KEY = -87.33


class At:

    def __init__(self, g, off, kind=None):
        self.g, self.off, self.kind = g, off, kind
        self.par = off % 2
        self.turn = g + off // 2 if not isinstance(g, int) or g else off // 2
        self.n = g * 2 + off if not isinstance(g, int) or g else off

    def __sub__(self, lag):
        return At(self.g, self.off - lag, self.kind)


def program(nc, x, ctx, ctxT, mask, gwT, w1, w2a, w2b, sim, out):
    table = nc.dram_tensor("list_table", (PAD_LIST + UNIT, 1), I32, kind="Internal").ap()
    normed = nc.dram_tensor("normed_tokens", (ROWS, ROW), F32, kind="Internal").ap()
    plan_d = nc.dram_tensor("plan_rows", (MAX_OVER, PCOLS), I32, kind="Internal").ap()

    with ExitStack() as stack:
        def sb(name, shape, dt=F32):
            return stack.enter_context(nc.sbuf_tensor(name, shape, dt))

        def two(name, shape, dt=F32):
            return [sb(f"{name}{i}", shape, dt) for i in range(2)]

        def rstd_tiles(name):
            return {k: sb(f"rstd_{name}_{k}", [T, 1]) for k in ("var", "log", "rough", "square", "half", "exact")}

        def sem(name):
            return stack.enter_context(nc.semaphore(name))

        def sem2(name):
            return [sem(f"{name}{i}") for i in range(2)]

        bank = [stack.enter_context(nc.psum_tensor(f"bank{i}", [P, 512], F32)) for i in range(8)]

        ident = sb("ident", [P, P])
        not_ident = sb("not_ident", [E, E])
        tri = sb("tri", [T, T], BF16)
        tri_incl = sb("tri_incl", [E, E], BF16)
        ident_b = sb("ident_b", [E, E], BF16)
        ones_b = sb("ones_b", [P, P], BF16)
        ones_f = sb("ones_f", [E, P])
        col_i = sb("col_i", [P, E], I32)
        col = sb("col", [P, E])
        list_base = sb("list_base", [P, E])
        thr_i = sb("thr_i", [P, E], I32)
        over_thr = sb("over_thr", [P, 12])
        pair_thr = sb("pair_thr", [P, E])
        row_i = sb("row_i", [P, 1], I32)
        row = sb("row", [P, 1])
        zeros = sb("zeros", [P, ROW])
        blank = sb("blank", [E, LIST // UNIT, UNIT], I32)
        sim_s = sb("sim_s", [E, E])
        gw_s = sb("gw_s", [P, DK, E])

        xa = two("x_for_norm", [T, D])
        xr = two("x_for_residual", [T, D])
        ctxT_s = two("ctxT_s", [P, DK, M])
        ctx_s = two("ctx_s", [MC, MK, D])
        mask_s = two("mask_s", [T, M], U8)
        st_a = sb("st_a", [T, 6]); mv_a = sb("mv_a", [T, 2]); rstd_a = rstd_tiles("a")
        xn = two("xn", [T, D])
        xnT = two("xnT", [P, DK, T])
        madd = two("madd", [T, M])
        shift_a = sb("shift_a", [T, 1]); shift_c = sb("shift_c", [T, 1])
        sc = two("scores", [T, M])
        nmax = two("nmax", [T, 1])
        pr = two("probs", [T, M])
        rsum = two("rsum", [T, 1])
        pT = two("probsT", [MC, MK, T])
        rinv = sb("rinv", [T, 1]); rval = sb("rval", [T, 1])
        st_c = sb("st_c", [T, 6]); mv_c = sb("mv_c", [T, 2]); rstd_c = rstd_tiles("c")
        x1 = two("x1", [T, D])
        xn2 = two("xn2", [T, D])
        xn2T = two("xn2T", [P, DK, T])
        lmax = sb("lmax", [T, 1])
        key = two("key", [T, E + NSENT])
        key8 = sb("key8", [T, TOPK])
        key4 = sb("key4", [T, TOPK])
        rest8 = sb("rest8", [T, E]); rest4 = sb("rest4", [T, E + NSENT])
        mk = two("mk", [T, 2, E], BF16)
        run = two("run", [T, 2, E], BF16)
        eall = two("eall", [T, E])
        esum = two("esum", [T, 1])
        einv = sb("einv", [T, 1]); pm = sb("pm", [T, E]); s8 = sb("s8", [T, 1])
        s8c = sb("s8c", [T, 1]); s8i = sb("s8i", [T, 1])
        wd = two("wd", [T, E])
        place = sb("place", [T, E]); placed = sb("placed", [T, E]); placed8 = sb("placed8", [T, TOPK])
        slot8 = two("slot8", [T, TOPK], I32)
        token = two("token", [T, 1], I32)

        prim = sb("prim", [E, E]); pen = sb("pen", [E, E]); simd = sb("simd", [E, E])
        sime = sb("sime", [E, E]); cand = sb("cand", [E, E]); candm = sb("candm", [E, E])
        best = sb("best", [E, 8]); bidx = sb("bidx", [E, 8], U32); bidxf = sb("bidxf", [E, 1])
        cp = sb("cp", [E, 1]); tot = sb("tot", [E, 1]); sec = sb("sec", [E, 1])
        rep = sb("rep", [E, 1]); repl = sb("repl", [E, 1]); diff = sb("diff", [E, 1])
        mapping = sb("mapping", [E, 1])
        over_is = sb("over_is", [E, 12]); nover = sb("nover", [E, 1])
        nover_b = sb("nover_b", [E, P], BF16); map_b = sb("map_b", [E, P], BF16)
        cum = sb("cum", [P, E]); le = sb("le", [P, E]); len_ = sb("len_", [P, E])
        eid = sb("eid", [P, 1]); pre = sb("pre", [P, 1])
        ohm = sb("ohm", [P, E]); ohs = sb("ohs", [P, E])
        rel = sb("rel", [P, 1]); relv = sb("relv", [P, 1]); real = sb("real", [P, 1])
        pairs_is = sb("pairs_is", [P, E])
        planf = sb("planf", [P, PCOLS])
        plani = sb("plani", [P, PCOLS], I32)
        prow = sb("prow", [1, MAX_OVER * PCOLS], I32)

        raw1 = two("raw1_", [P, DK * 2 * F])
        raw2 = two("raw2_", [P, 2, D])
        w1h = two("w1h", [P, DK, 2 * F], F32R)
        w1l = two("w1l", [P, DK, 2 * F], F32R)
        w2h = two("w2h", [P, 2, D], F32R)
        w2l = two("w2l", [P, D], F32R)
        lg = two("list_for_gather", [P, 2], I32)
        lists = [two("list_held", [P, 2], I32), two("list_passed", [P, 2], I32)]
        ls = two("list_for_scatter", [P, 2], I32)
        xg = two("xg", [P, 2, ROW])
        wt_early = two("wt_early", [P, 2]); wt = two("wt", [P, 2])
        xh = two("xh", [P, DK, UNIT], F32R)
        xl = two("xl", [P, DK, UNIT], F32R)
        sg = sb("sg", [P, 2, UNIT])
        h = sb("h", [P, 2, UNIT])
        hh = two("hh", [P, 2, UNIT], F32R)
        hl = two("hl", [P, 2, UNIT], F32R)
        ys = two("ys", [P, 2, D])

        const_pool = sem("const_pool"); const_dve = sem("const_dve"); const_in = sem("const_in")
        filled = sem("filled")
        x_in = sem2("x_in"); xr_in = sem2("xr_in"); ctxT_in = sem2("ctxT_in"); ctx_in = sem2("ctx_in")
        mask_in = sem2("mask_in")
        x1_out = sem2("x1_out"); xn2_out = sem2("xn2_out")
        c_norm = sem("c_norm"); c_normed = sem("c_normed"); c_renorm = sem("c_renorm"); xn_s = sem("xn_s"); xn2_s = sem("xn2_s"); madd_s = sem("madd_s"); wd_out = sem2("wd_out"); wt_early_s = sem("wt_early_s"); wt_s = sem("wt_s"); c_score = sem("c_score"); c_resid = sem("c_resid")
        c_top = sem("c_top"); c_place = sem("c_place")
        xnT_ps = sem("xnT_ps"); score_ps = sem("score_ps"); pT_ps = sem("pT_ps"); read_ps = sem("read_ps")
        xn2T_ps = sem("xn2T_ps"); logit_ps = sem("logit_ps"); place_ps = sem("place_ps")
        xnT_sb = sem("xnT_sb"); probs_sb = sem("probs_sb"); pT_sb = sem("pT_sb"); xn2T_sb = sem("xn2T_sb")
        exps_sb = sem("exps_sb"); rough_a = sem("rough_a"); rough_c = sem("rough_c")
        tabled = sem2("tabled")
        plan_ps = sem("plan_ps"); c_plan = sem("c_plan"); plan_out = sem("plan_out"); plan_in = sem("plan_in")
        w1_in = sem2("w1_in"); w2_in = sem2("w2_in"); lg_in = sem2("lg_in");
        held_s = sem("held_s"); passed_s = sem("passed_s"); taken_s = sem("taken_s")
        gathered = sem2("gathered"); scattered = sem("scattered")
        w1h_s = sem("w1h_s"); w1l_s = sem("w1l_s"); w2h_s = sem("w2h_s"); w2l_s = sem("w2l_s")
        xT_ps = sem("xT_ps"); gu_ps = sem("gu_ps"); hT_ps = sem("hT_ps"); y_ps = sem("y_ps")
        xh_s = sem("xh_s"); xl_s = sem("xl_s"); silu_s = sem("silu_s"); h_s = sem("h_s")
        hh_s = sem("hh_s"); hl_s = sem("hl_s"); ys_s = sem("ys_s")
        cleared = sem("cleared"); spacer = sem("spacer")

        NORM, NORMED, SCORE, RESID, RENORM, TOP, PLACE = 3, 4, 2, 6, 4, 9, 11

        def split_wait(eng, s, value):
            wait(eng, s, value)
            if not isinstance(value, int):
                eng.sem_inc(spacer, 1)

        def wait(eng, s, value):
            if not isinstance(value, int) or value > 0:
                eng.wait_ge(s, value)

        class Chain:
            def __init__(self, eng, s, links, n):
                self.eng, self.s, self.links, self.base, self.c = eng, s, links, n * links, 0

            def link(self, ins, alone=False):
                self.c += 1
                ins.then_inc(self.s, 1)
                yield
                if self.c < self.links:
                    (split_wait if alone else wait)(self.eng, self.s, self.base + self.c)

            def done(self):
                assert self.c == self.links, (self.c, self.links)

        def taking_turns(slot, *stages):
            going = []
            batches(slot, *((lag, lambda b, stage=stage: going.append(stage(b))) for lag, stage in stages))
            while going:
                going = [chain for chain in going if next(chain, "ended") != "ended"]

        def phase1(eng, body):
            for n in range(-2, 6):
                body(At(0, n))
            with eng.Fori(3, 7) as g:
                for j in range(2):
                    body(At(g, j))
            for n in range(14, 21):
                body(At(0, n))

        def batches(slot, *stages):
            for lag, stage in stages:
                b = slot - lag
                if not isinstance(b.g, int) or 0 <= b.off < B:
                    stage(b)

        def phase2(eng, pairs, body):
            for n in range(-3, 4):
                body(At(0, n))
            with eng.Fori(2, 30) as g:
                for j in range(2):
                    body(At(g, j, "main"))
            for n in range(60, 68):
                body(At(0, n))
            with eng.Fori(34, pairs + 32) as g:
                for j in range(2):
                    body(At(g, j, "over"))
            for j in range(2):
                body(At(pairs + 32, j, "last"))

        def units(slot, *stages):
            for lag, stage in stages:
                u = slot - lag
                if slot.kind == "last" and u.off >= 0:
                    continue
                if slot.kind is None:
                    if u.off < 0:
                        continue
                    u.kind = "main" if u.off < E else "over"
                if u.kind == "last":
                    u.kind = "over"
                stage(u)

        def only(kind, stage):
            def do(u):
                if u.kind == kind:
                    stage(u)
            return do

        def tiles(u):
            return 2 if u.kind == "main" else 1

        def upto(u, back):
            if u.kind == "main" or (isinstance(u.g, int) and u.off - back < E):
                return (u.n - back + 1) * 2
            return u.n - back + 1 + E

        def before(u):
            return upto(u, 1)

        def before_par(u):
            return u.turn * 2 if u.kind == "main" else u.turn + E // 2

        def turned(u):
            return bank[2 + u.par][:, 0:2 * P].rearrange("p (k t) -> p k t", k=2)

        def pairs_of(eng):
            eng.wait_ge(plan_in, 16)
            return eng.value_load(prow[0:1, 3:4], min_val=3, max_val=59)

        block = stack.enter_context(nc.Block())

        @block.sync
        def _(sp):
            sp.dma_start(gw_s[:], gwT).then_inc(const_in, 16)
            sp.dma_start(sim_s[:], sim).then_inc(const_in, 16)

            def load_early(b):
                split_wait(sp, xn_s, b.n - 1)
                sp.dma_start(xa[b.par][:], x[bass.ds(b.n, 1)].rearrange("a t d -> (a t) d")).then_inc(x_in[b.par], 16)
                split_wait(sp, score_ps, b.n - 1)
                sp.dma_start(ctxT_s[b.par][:], ctxT[bass.ds(b.n, 1)].rearrange("a p c m -> (a p) c m")).then_inc(ctxT_in[b.par], 16)
                split_wait(sp, madd_s, b.n - 1)
                sp.dma_start(mask_s[b.par][:], mask[bass.ds(b.n, 1)].broadcast_to([T, M])).then_inc(mask_in[b.par], 16)

            def load_late(b):
                split_wait(sp, read_ps, b.n - 1)
                sp.dma_start(ctx_s[b.par][:], ctx[bass.ds(b.n, 1)].rearrange("a (c p) d -> (a p) c d", p=MC)).then_inc(ctx_in[b.par], 16)
                split_wait(sp, c_resid, (b.n - 1) * RESID)
                sp.dma_start(xr[b.par][:], x[bass.ds(b.n, 1)].rearrange("a t d -> (a t) d")).then_inc(xr_in[b.par], 16)

            def store(b):
                split_wait(sp, c_resid, b.n * RESID + 3)
                sp.dma_start(out[bass.ds(b.n * T, T), :], x1[b.par][:]).then_inc(x1_out[b.par], 16)

            def store_normed(b):
                split_wait(sp, xn2_s, b.n + 1)
                sp.dma_start(normed[bass.ds(b.n * T, T), 0:D], xn2[b.par][:]).then_inc(xn2_out[b.par], 16)

            def store_weights(b):
                split_wait(sp, c_place, b.n * PLACE + 6)
                sp.dma_start(normed[bass.ds(b.n * T, T), D:ROW], wd[b.par][:]).then_inc(wd_out[b.par], 16)

            def fill(b):
                sp.wait_ge(const_pool, 1)
                sp.dma_start(out[TOK:TOK + P, :], zeros[:, 0:D]).then_inc(filled, 16)
                sp.dma_start(out[TOK + P:ROWS, :], zeros[:, 0:D]).then_inc(filled, 16)
                sp.dma_start(normed[TOK:TOK + P, :], zeros[:]).then_inc(filled, 16)
                sp.dma_start(normed[TOK + P:ROWS, :], zeros[:]).then_inc(filled, 16)
                sp.wait_ge(const_pool, 2)
                sp.dma_start(table[0:PAD_LIST].rearrange("(e n) c -> e (n c)", e=E),
                             blank[:].rearrange("e a b -> e (a b)")).then_inc(filled, 16)
                sp.dma_start(table[PAD_LIST:PAD_LIST + UNIT].rearrange("(o n) c -> o (n c)", o=1),
                             blank[0:1, 0]).then_inc(filled, 16)

            def slot(s):
                batches(s, (-2, load_early), (-1, load_late))
                if isinstance(s.g, int) and s.off == -1:
                    fill(s)
                batches(s, (2, store_normed), (4, store_weights), (1, store))

            phase1(sp, slot)

            sp.wait_ge(c_plan, PLAN)
            sp.dma_start(plan_d, plani[:]).then_inc(plan_out, 16)
            sp.wait_ge(plan_out, 16)
            sp.dma_start(prow[:], plan_d.rearrange("(o r) c -> o (r c)", o=1)).then_inc(plan_in, 16)
            pairs = pairs_of(sp)
            for p in range(2):
                sp.wait_ge(tabled[p], B // 2 * TOPK * 16)

            def expert(u):
                if u.kind == "main":
                    return sp.value_load(prow[0:1, bass.ds(u.n * PCOLS + 2, 1)], min_val=0, max_val=E - 1)
                return sp.value_load(prow[0:1, bass.ds((u.n - E) * PCOLS, 1)], min_val=0, max_val=E - 1)

            def first_entry(u):
                if u.kind == "main":
                    return u.n * LIST
                return sp.value_load(prow[0:1, bass.ds((u.n - E) * PCOLS + 1, 1)], min_val=0, max_val=PAD_LIST)

            def load_list(u, dst, s):
                n = tiles(u)
                rows = table[bass.ds(first_entry(u), n * P), :].rearrange("(p t) c -> p (t c)", p=P)
                sp.dma_start(dst[u.par][:, 0:n], rows).then_inc(s[u.par], 16)

            def load_w1(u):
                split_wait(sp, w1h_s, u.n - 1)
                split_wait(sp, w1l_s, u.n - 1)
                sp.dma_start(raw1[u.par][:], w1[bass.ds(expert(u), 1)].rearrange("a p f -> (a p) f")).then_inc(w1_in[u.par], 16)

            def load_w2(u):
                split_wait(sp, w2h_s, u.n - 1)
                split_wait(sp, w2l_s, u.n - 1)
                e = expert(u)
                sp.dma_start(raw2[u.par][:, 0, :], w2a[bass.ds(e, 1)].rearrange("a p f -> (a p) f")).then_inc(w2_in[u.par], 16)
                sp.dma_start(raw2[u.par][0:FR, 1, :], w2b[bass.ds(e, 1)].rearrange("a p f -> (a p) f")).then_inc(w2_in[u.par], 16)

            def load_for_gather(u):
                split_wait(sp, gathered[u.par], before_par(u) * 16)
                split_wait(sp, held_s, u.n - 1)
                load_list(u, lg, lg_in)

            def slot2(s):
                units(s, (-2, load_w1), (-3, load_for_gather), (-1, load_w2))

            phase2(sp, pairs, slot2)
            n = pairs * 2 + E
            split_wait(sp, scattered, (pairs * 2 + 2 * E) * 16)
            for p in range(2):
                split_wait(sp, w1_in[p], (pairs + E // 2 + 1) * 16)
                split_wait(sp, gathered[p], (pairs + E // 2 + 1 + E // 2) * 16)
            split_wait(sp, w2_in[0], (pairs + E // 2 + 1) * 32)
            split_wait(sp, lg_in[0], (pairs + E // 2 + 2 - 1) * 16)
            split_wait(sp, lg_in[1], (pairs + E // 2 + 1) * 16)
            split_wait(sp, lg_in[0], (pairs + E // 2 + 2) * 16)

        @block.gpsimd
        def _(pool):
            nc.gpsimd.memset(zeros[:], 0.0).then_inc(const_pool, 1)
            nc.gpsimd.iota(blank[:], [[0, LIST // UNIT], [1, UNIT]], base=TOK,
                           channel_multiplier=0).then_inc(const_pool, 1)
            nc.gpsimd.memset(ident[:], 0.0).then_inc(cleared, 1)
            nc.gpsimd.memset(tri[:], 1.0).then_inc(cleared, 1)
            nc.gpsimd.memset(tri_incl[:], 1.0).then_inc(cleared, 1)
            nc.gpsimd.memset(ident_b[:], 0.0).then_inc(cleared, 1)
            pool.wait_ge(cleared, 4)
            nc.gpsimd.affine_select(out=ident[:], in_=ident[:], compare_op=ALU.not_equal, fill=1.0, base=0,
                                    pattern=[[-1, P]], channel_multiplier=1).then_inc(const_pool, 1)
            nc.gpsimd.affine_select(out=tri[:], in_=tri[:], compare_op=ALU.is_gt, fill=0.0, base=0,
                                    pattern=[[1, T]], channel_multiplier=-1).then_inc(const_pool, 1)
            nc.gpsimd.affine_select(out=tri_incl[:], in_=tri_incl[:], compare_op=ALU.is_ge, fill=0.0, base=0,
                                    pattern=[[1, E]], channel_multiplier=-1).then_inc(const_pool, 1)
            nc.gpsimd.affine_select(out=ident_b[:], in_=ident_b[:], compare_op=ALU.not_equal, fill=1.0, base=0,
                                    pattern=[[-1, E]], channel_multiplier=1).then_inc(const_pool, 1)
            nc.gpsimd.memset(ones_b[:], 1.0).then_inc(const_pool, 1)
            nc.gpsimd.memset(ones_f[:], 1.0).then_inc(const_pool, 1)
            nc.gpsimd.iota(col_i[:], [[1, E]], base=0, channel_multiplier=0).then_inc(const_pool, 1)
            nc.gpsimd.iota(row_i[:], [[0, 1]], base=0, channel_multiplier=1).then_inc(const_pool, 1)
            for p in range(2):
                nc.gpsimd.iota(token[p][:], [[0, 1]], base=T * (p - 2), channel_multiplier=1).then_inc(const_pool, 1)
                for i in range(NSENT):
                    nc.gpsimd.memset(key[p][:, E + i:E + i + 1], float(i + 1)).then_inc(const_pool, 1)
            for i in range(NSENT):
                nc.gpsimd.memset(key4[:, SELK + i:SELK + i + 1], float(i + 1)).then_inc(const_pool, 1)
            nc.gpsimd.memset(planf[:], 0.0).then_inc(const_pool, 1)
            nc.gpsimd.memset(run[0][:], 0.0).then_inc(const_pool, 1)
            nc.gpsimd.memset(sg[:], 0.0).then_inc(const_pool, 1)

            pool.wait_ge(filled, 6 * 16)

            def enter(b):
                split_wait(pool, c_place, (b.n + 1) * PLACE)
                for k in range(TOPK):
                    pool.indirect_dma_start(table, bass.IndirectOffsetOnAxis(ap=slot8[b.par][:, k:k + 1], axis=0),
                                            token[b.par][:], None).then_inc(tabled[b.par], 16)

            phase1(pool, lambda s: batches(s, (4, enter)))

            pairs = pairs_of(pool)
            for p in range(2):
                pool.wait_ge(xn2_out[p], B // 2 * 16)
                pool.wait_ge(wd_out[p], B // 2 * 16)
                pool.wait_ge(x1_out[p], B // 2 * 16)

            def gather(u):
                split_wait(pool, lg_in[u.par], (u.turn + 1) * 16)
                split_wait(pool, xT_ps, upto(u, 2))
                split_wait(pool, wt_early_s, upto(u, 2))
                split_wait(pool, passed_s, u.n - 1)
                n = tiles(u)
                nc.gpsimd.tensor_copy(lists[0][u.par][:, 0:n], lg[u.par][:, 0:n]).then_inc(held_s, 1)
                for t in range(tiles(u)):
                    pool.indirect_dma_start(xg[u.par][:, t, :], None, normed,
                                            bass.IndirectOffsetOnAxis(ap=lg[u.par][:, t:t + 1], axis=0)
                                            ).then_inc(gathered[u.par], 16)

            def weights_early(u):
                split_wait(pool, gathered[u.par], (before_par(u) + tiles(u)) * 16)
                split_wait(pool, wt_s, u.n - 1)
                if u.kind == "main":
                    e = u.n
                else:
                    e = pool.value_load(prow[0:1, bass.ds((u.n - E) * PCOLS + 4, 1)], min_val=0, max_val=E - 1)
                n = tiles(u)
                nc.gpsimd.tensor_copy(wt_early[u.par][:, 0:n], xg[u.par][:, 0:n, bass.ds(e + D, 1)].rearrange("p t o -> p (t o)")
                                      ).then_inc(wt_early_s, n)

            def hand_list(u):
                split_wait(pool, held_s, u.n + 1)
                split_wait(pool, taken_s, u.n - 1)
                n = tiles(u)
                nc.gpsimd.tensor_copy(lists[1][u.par][:, 0:n], lists[0][u.par][:, 0:n]).then_inc(passed_s, 1)

            def take_list(u):
                split_wait(pool, passed_s, u.n + 1)
                split_wait(pool, scattered, upto(u, 2) * 16)
                n = tiles(u)
                nc.gpsimd.tensor_copy(ls[u.par][:, 0:n], lists[1][u.par][:, 0:n]).then_inc(taken_s, 1)

            def scatter(u):
                split_wait(pool, taken_s, u.n + 1)
                split_wait(pool, ys_s, before(u) + tiles(u))
                split_wait(pool, scattered, before(u) * 16)
                for t in range(tiles(u)):
                    pool.indirect_dma_start(out, bass.IndirectOffsetOnAxis(ap=ls[u.par][:, t:t + 1], axis=0),
                                            ys[u.par][:, t, :], None, compute_op=ALU.add).then_inc(scattered, 16)

            phase2(pool, pairs, lambda s: units(s, (2, take_list), (0, hand_list), (0, weights_early), (-2, gather), (2, scatter)))

        @block.vector
        def _(dve):
            v = nc.vector
            dve.wait_ge(const_pool, CONSTS)
            v.tensor_copy(col[:], col_i[:]).then_inc(const_dve, 1)
            v.tensor_copy(row[:], row_i[:]).then_inc(const_dve, 1)
            v.tensor_scalar(not_ident[:], ident[0:E, 0:E], -1.0, 1.0, ALU.mult, ALU.add).then_inc(const_dve, 1)
            dve.wait_ge(const_dve, 3)
            v.tensor_scalar(list_base[:], col[:], -float(LIST), float(PAD_LIST), ALU.mult, ALU.add).then_inc(const_dve, 1)
            v.tensor_scalar(over_thr[:], col[:, 0:12], float(OVER), float(UNIT), ALU.mult, ALU.add).then_inc(const_dve, 1)
            v.tensor_scalar(pair_thr[:], col[:], 2.0, 6.0, ALU.mult, ALU.add).then_inc(const_dve, 1)
            dve.wait_ge(const_dve, 6)

            def norm(b):
                ch = Chain(dve, c_norm, NORM, b.n)
                dve.wait_ge(x_in[b.par], (b.turn + 1) * 16)
                wait(dve, xn_s, b.n)
                yield from ch.link(v.bn_stats(st_a[:], xa[b.par][:]), alone=True)
                yield from ch.link(v.bn_aggr(mv_a[:], st_a[:]))
                yield from ch.link(v.tensor_scalar(rstd_a["var"][:], mv_a[:, 1:2], EPS, None, ALU.add))
                ch.done()

            def newton(ch, r):
                yield from ch.link(v.tensor_tensor(r["square"][:], r["rough"][:], r["rough"][:], ALU.mult))
                yield from ch.link(v.tensor_scalar(r["half"][:], r["square"][:], r["var"][:], -0.5, ALU.mult, ALU.mult))
                yield from ch.link(v.scalar_tensor_tensor(r["exact"][:], r["half"][:], 1.5, r["rough"][:], ALU.add, ALU.mult))

            def normed_x(b):
                ch = Chain(dve, c_normed, NORMED, b.n)
                dve.wait_ge(rough_a, (b.n + 1) * 2)
                yield from newton(ch, rstd_a)
                yield from ch.link(v.tensor_scalar(shift_a[:], mv_a[:, 0:1], -1.0, rstd_a["exact"][:], ALU.mult, ALU.mult))
                ch.done()

            def norm_and_scale(b):
                yield from norm(b)
                yield from normed_x(b)

            def score(b):
                ch = Chain(dve, c_score, SCORE, b.n)
                dve.wait_ge(madd_s, b.n + 1)
                dve.wait_ge(score_ps, b.n + 1)
                wait(dve, probs_sb, b.n - 1)
                wait(dve, c_resid, (b.n - 1) * RESID)
                yield from ch.link(v.scalar_tensor_tensor(sc[b.par][:], bank[1][0:T, 0:M], SCALE, madd[b.par][:], ALU.mult, ALU.add))
                yield from ch.link(v.tensor_reduce(nmax[b.par][:], sc[b.par][:], AX, ALU.max, negate=True))
                ch.done()

            def resid(b):
                ch = Chain(dve, c_resid, RESID, b.n)
                dve.wait_ge(probs_sb, b.n + 1)
                yield from ch.link(v.reciprocal(rinv[:], rsum[b.par][:]))
                yield from ch.link(v.tensor_scalar(rval[:], nmax[b.par][:], NEG / 2, rinv[:], ALU.is_lt, ALU.mult))
                dve.wait_ge(xr_in[b.par], (b.turn + 1) * 16)
                dve.wait_ge(read_ps, b.n + 1)
                wait(dve, x1_out[b.par], b.turn * 16)
                wait(dve, xn2_s, b.n - 1)
                yield from ch.link(v.scalar_tensor_tensor(x1[b.par][:], bank[3][0:T, :], rval[:], xr[b.par][:], ALU.mult, ALU.add))
                yield from ch.link(v.bn_stats(st_c[:], x1[b.par][:]), alone=True)
                yield from ch.link(v.bn_aggr(mv_c[:], st_c[:]))
                yield from ch.link(v.tensor_scalar(rstd_c["var"][:], mv_c[:, 1:2], EPS, None, ALU.add))
                ch.done()

            def renormed_x(b):
                ch = Chain(dve, c_renorm, RENORM, b.n)
                dve.wait_ge(rough_c, (b.n + 1) * 2)
                wait(dve, xn2_s, b.n)
                yield from newton(ch, rstd_c)
                yield from ch.link(v.tensor_scalar(shift_c[:], mv_c[:, 0:1], -1.0, rstd_c["exact"][:], ALU.mult, ALU.mult))
                ch.done()

            def top(b):
                ch = Chain(dve, c_top, TOP, b.n)
                dve.wait_ge(logit_ps, b.n + 1)
                yield from ch.link(v.tensor_reduce(lmax[:], bank[5][0:T, 0:E], AX, ALU.max))
                wait(dve, exps_sb, b.n - 1)
                k = key[b.par]
                yield from ch.link(v.tensor_scalar(k[:, 0:E], bank[5][0:T, 0:E], lmax[:], LOW_KEY, ALU.subtract, ALU.max), alone=True)
                yield from ch.link(v.max(key8[:], k[:, 0:E]), alone=True)
                yield from ch.link(v.tensor_copy(key4[:, 0:SELK], key8[:, 0:SELK]), alone=True)
                yield from ch.link(v.match_replace(rest8[:], key8[:], k[:, 0:E], 5.0), alone=True)
                yield from ch.link(v.match_replace(rest4[:], key4[:], k[:], 5.0))
                wait(dve, place_ps, b.n - 1)
                wait(dve, c_place, (b.n - 1) * PLACE)
                yield from ch.link(v.tensor_scalar(mk[b.par][:, 0, :], rest4[:, 0:E], 4.5, None, ALU.is_gt))
                yield from ch.link(v.tensor_scalar(mk[b.par][:, 1, :], rest8[:], 4.5, None, ALU.is_gt))
                wait(dve, place_ps, b.n)
                yield from ch.link(v.tensor_tensor(run[1 - b.par][:], run[b.par][:], mk[b.par][:], ALU.add))
                ch.done()

            def place_entries(b):
                ch = Chain(dve, c_place, PLACE, b.n)
                dve.wait_ge(exps_sb, b.n + 1)
                yield from ch.link(v.reciprocal(einv[:], esum[b.par][:]))
                yield from ch.link(v.scalar_tensor_tensor(pm[:], eall[b.par][:], einv[:], mk[b.par][:, 1, :], ALU.mult, ALU.mult))
                yield from ch.link(v.tensor_reduce(s8[:], pm[:], AX, ALU.add))
                yield from ch.link(v.tensor_scalar(s8c[:], s8[:], 1e-12, None, ALU.max))
                yield from ch.link(v.reciprocal(s8i[:], s8c[:]))
                wait(dve, wd_out[b.par], b.turn * 16)
                yield from ch.link(v.tensor_scalar(wd[b.par][:], pm[:], s8i[:], None, ALU.mult))
                dve.wait_ge(place_ps, b.n + 1)
                yield from ch.link(v.tensor_tensor(place[:], list_base[0:T, :], bank[6][0:T, 0:E], ALU.subtract))
                yield from ch.link(v.tensor_tensor(placed[:], place[:], mk[b.par][:, 1, :], ALU.mult), alone=True)
                yield from ch.link(v.max(placed8[:], placed[:]))
                wait(dve, tabled[b.par], b.turn * TOPK * 16)
                yield from ch.link(v.tensor_scalar(slot8[b.par][:], placed8[:], -1.0, float(PAD_LIST), ALU.mult, ALU.add))
                yield from ch.link(v.tensor_scalar(token[b.par][:], token[b.par][:], 2 * T, None, ALU.add))
                ch.done()

            def slot(s):
                taking_turns(s, (4, place_entries), (3, top), (-1, norm_and_scale), (2, renormed_x))
                taking_turns(s, (0, score))
                taking_turns(s, (1, resid))

            phase1(dve, slot)

            ch = Chain(dve, c_plan, PLAN, 0)

            def step(ins):
                for _ in ch.link(ins):
                    pass

            dve.wait_ge(const_in, 32)
            dve.wait_ge(plan_ps, 1)
            step(v.tensor_scalar(prim[:], bank[7][0:E, 0:E], 0.0, None, ALU.is_gt))
            step(v.tensor_copy(cp[:], bank[7][0:E, 64:65]))
            step(v.tensor_copy(tot[:], bank[7][0:E, 80:81]))
            step(v.tensor_tensor(simd[:], sim_s[:], not_ident[:], ALU.mult))
            step(v.tensor_tensor(sime[:], simd[:], ident[0:E, 0:E], ALU.add))
            step(v.tensor_tensor(candm[:], sime[:], prim[:], ALU.mult))
            step(v.tensor_scalar(pen[:], prim[:], -1.0, NEG, ALU.add, ALU.mult))
            step(v.tensor_tensor(cand[:], candm[:], pen[:], ALU.add))
            step(v.max(best[:], cand[:]))
            step(v.max_index(bidx[:], best[:], cand[:]))
            step(v.tensor_copy(bidxf[:], bidx[:, 0:1]))
            step(v.tensor_tensor(sec[:], tot[:], cp[:], ALU.is_gt))
            step(v.tensor_scalar(rep[:], cp[:], 0.0, sec[:], ALU.is_le, ALU.mult))
            step(v.tensor_scalar(repl[:], best[:, 0:1], THRESH, rep[:], ALU.is_ge, ALU.mult))
            step(v.tensor_tensor(diff[:], bidxf[:], row[0:E], ALU.subtract))
            step(v.scalar_tensor_tensor(mapping[:], diff[:], repl[:], row[0:E], ALU.mult, ALU.add))
            step(v.tensor_scalar(over_is[:], over_thr[0:E, :], tot[:], None, ALU.is_lt))
            step(v.tensor_reduce(nover[:], over_is[:], AX, ALU.add))
            step(v.tensor_scalar(nover_b[:], ones_f[:], nover[:], None, ALU.mult))
            step(v.tensor_scalar(map_b[:], ones_f[:], mapping[:], None, ALU.mult))
            assert ch.c == PLAN_A
            dve.wait_ge(plan_ps, 2)
            step(v.tensor_scalar(le[:], bank[7][:, 128:192], row[:], None, ALU.is_le))
            step(v.tensor_reduce(eid[:], le[:], AX, ALU.add))
            step(v.tensor_tensor(len_[:], bank[7][:, 192:256], le[:], ALU.mult))
            step(v.tensor_reduce(pre[:], len_[:], AX, ALU.add))
            step(v.tensor_scalar(ohs[:], col[:], eid[:], None, ALU.is_equal))
            step(v.tensor_tensor(ohm[:], bank[7][:, 256:320], ohs[:], ALU.mult))
            step(v.tensor_reduce(planf[:, 0:1], ohm[:], AX, ALU.add))
            step(v.tensor_tensor(rel[:], row[:], pre[:], ALU.subtract))
            step(v.tensor_scalar(relv[:], rel[:], float(OVER), float(UNIT), ALU.mult, ALU.add))
            step(v.tensor_scalar(real[:], eid[:], float(E), relv[:], ALU.is_lt, ALU.mult))
            step(v.scalar_tensor_tensor(planf[:, 1:2], eid[:], float(LIST), real[:], ALU.mult, ALU.add))
            step(v.tensor_copy(planf[0:E, 2:3], mapping[:]))
            step(v.tensor_copy(cum[:], bank[7][:, 128:192]))
            step(v.tensor_scalar(pairs_is[:], pair_thr[:], cum[:, E - 1:E], None, ALU.is_lt))
            step(v.tensor_reduce(pre[:], pairs_is[:], AX, ALU.add))
            step(v.tensor_scalar(planf[:, 3:4], pre[:], 3.0, None, ALU.add))
            step(v.tensor_scalar(planf[:, 4:5], eid[:], float(E - 1), None, ALU.min))
            step(v.tensor_copy(plani[:], planf[:]))
            ch.done()

            pairs = pairs_of(dve)

            def h_products(u):
                W = tiles(u) * P
                dve.wait_ge(silu_s, (u.n + 1) * 2)
                dve.wait_ge(gu_ps, u.n + 1)
                wait(dve, hh_s, u.n)
                wait(dve, hl_s, u.n)
                ab, c = bank[u.par], bank[2 + u.par]
                if u.kind == "over":
                    last = slice(2 * P + FR, 2 * P + 2 * FR)
                    v.tensor_tensor(h[:, 0, 0:P], sg[:, 0, 0:P], ab[:, P:2 * P], ALU.mult).then_inc(h_s, 1)
                    v.tensor_tensor(h[:, 0, P:F], sg[:, 0, P:F], ab[:, last], ALU.mult).then_inc(h_s, 1)
                    v.tensor_tensor(h[:, 0, F:2 * P], sg[:, 0, P:F], ab[:, last], ALU.mult).then_inc(h_s, 1)
                    return
                v.tensor_tensor(h[:, 0, 0:W], sg[:, 0, 0:W], ab[:, UNIT:UNIT + W], ALU.mult).then_inc(h_s, 1)
                v.tensor_tensor(h[0:FR, 1, 0:W], sg[0:FR, 1, 0:W], c[FR:P, 0:W], ALU.mult).then_inc(h_s, 1)
                v.tensor_tensor(h[FR:P, 1, 0:W], sg[0:FR, 1, 0:W], c[FR:P, 0:W], ALU.mult).then_inc(h_s, 1)

            def h_low(u):
                W = tiles(u) * P
                dve.wait_ge(hh_s, u.n + 1)
                wait(dve, y_ps, upto(u, 2))
                src = turned(u) if u.kind == "over" else h[:, :, 0:W]
                v.tensor_tensor(hl[u.par][:, :, 0:W], src, hh[u.par][:, :, 0:W].bitcast(F32),
                                ALU.subtract).then_inc(hl_s, 1)

            def x_low(u):
                wait(dve, gu_ps, u.n - 1)
                for t in range(tiles(u)):
                    dve.wait_ge(xh_s, before(u) + t + 1)
                    v.tensor_tensor(xl[u.par][:, :, t * P:(t + 1) * P], bank[6 + t][:].rearrange("p (c t) -> p c t", c=DK),
                                    xh[u.par][:, :, t * P:(t + 1) * P].bitcast(F32), ALU.subtract).then_inc(xl_s, 1)

            def w1_low(u):
                dve.wait_ge(w1h_s, u.n + 1)
                wait(dve, gu_ps, u.n - 1)
                v.tensor_tensor(w1l[u.par][:].rearrange("p c f -> p (c f)"), raw1[u.par][:],
                                w1h[u.par][:].rearrange("p c f -> p (c f)").bitcast(F32), ALU.subtract).then_inc(w1l_s, 1)

            def w2_low(u):
                dve.wait_ge(w2h_s, u.n + 1)
                wait(dve, y_ps, upto(u, 2))
                v.tensor_tensor(w2l[u.par][:], raw2[u.par][:, 0, :], w2h[u.par][:, 0, :].bitcast(F32), ALU.subtract)
                v.tensor_tensor(w2h[u.par][FR:P, 1, :], raw2[u.par][0:FR, 1, :], w2h[u.par][0:FR, 1, :].bitcast(F32),
                                ALU.subtract).then_inc(w2l_s, 1)

            def weights(u):
                wait(dve, wt_early_s, before(u) + tiles(u))
                wait(dve, ys_s, upto(u, 2))
                v.tensor_copy(wt[u.par][:, 0:tiles(u)], wt_early[u.par][:, 0:tiles(u)]).then_inc(wt_s, 1)

            phase2(dve, pairs, lambda s: units(
                s, (1, weights), (1, h_products), (1, only("over", w2_low)), (1, only("over", h_low)), (-1, w1_low),
                (1, only("main", h_low)), (-1, x_low), (0, only("main", w2_low))))

        @block.scalar
        def _(act):
            a = nc.scalar

            def copy_pT(b):
                act.wait_ge(pT_ps, b.n + 1)
                wait(act, read_ps, b.n - 1)
                a.copy(pT[b.par][:], bank[2][0:MC, 0:MK * T].rearrange("p (c t) -> p c t", c=MK)).then_inc(pT_sb, 1)

            def copy_xn2T(b):
                act.wait_ge(xn2T_ps, b.n + 1)
                wait(act, logit_ps, b.n - 1)
                a.copy(xn2T[b.par][:], bank[4][:, 0:DK * T].rearrange("p (c t) -> p c t", c=DK)).then_inc(xn2T_sb, 1)

            def exps(b):
                act.wait_ge(c_top, b.n * TOP + 2)
                wait(act, c_place, (b.n - 1) * PLACE)
                a.activation(eall[b.par][:], key[b.par][:, 0:E], ACT.Exp, accum_out=esum[b.par][:]).then_inc(exps_sb, 1)

            def mask_add(b):
                act.wait_ge(mask_in[b.par], (b.turn + 1) * 16)
                wait(act, c_score, (b.n - 1) * SCORE)
                a.activation(madd[b.par][:], mask_s[b.par][:], ACT.Copy, scale=NEG, bias=-NEG).then_inc(madd_s, 1)

            def norm_x(b):
                act.wait_ge(c_normed, (b.n + 1) * NORMED)
                wait(act, xnT_ps, b.n - 1)
                a.activation(xn[b.par][:], xa[b.par][:], ACT.Identity, bias=shift_a[:], scale=rstd_a["exact"][:]).then_inc(xn_s, 1)

            def norm_x1(b):
                act.wait_ge(c_renorm, (b.n + 1) * RENORM)
                wait(act, xn2T_ps, b.n - 1)
                wait(act, xn2_out[b.par], b.turn * 16)
                a.activation(xn2[b.par][:], x1[b.par][:], ACT.Identity, bias=shift_c[:], scale=rstd_c["exact"][:]).then_inc(xn2_s, 1)

            def exp_scores(b):
                act.wait_ge(c_score, (b.n + 1) * SCORE)
                wait(act, c_resid, (b.n - 1) * RESID)
                wait(act, pT_ps, b.n - 1)
                a.activation(pr[b.par][:], sc[b.par][:], ACT.Exp, bias=nmax[b.par][:],
                             accum_out=rsum[b.par][:]).then_inc(probs_sb, 1)

            def copy_xnT(b):
                act.wait_ge(xnT_ps, b.n + 1)
                wait(act, score_ps, b.n - 1)
                a.copy(xnT[b.par][:], bank[0][:, 0:DK * T].rearrange("p (c t) -> p c t", c=DK)).then_inc(xnT_sb, 1)

            def rough(s, c, links, r):
                def stage(b):
                    act.wait_ge(c, (b.n + 1) * links)
                    a.activation(r["log"][:], r["var"][:], ACT.Ln).then_inc(s, 1)
                    act.wait_ge(s, b.n * 2 + 1)
                    a.activation(r["rough"][:], r["log"][:], ACT.Exp, scale=-0.5).then_inc(s, 1)
                return stage

            nc.scalar.preload_act_table_set("natural_log_exp_and_others")
            phase1(act, lambda s: batches(s, (1, copy_pT), (-1, rough(rough_a, c_norm, NORM, rstd_a)), (2, norm_x1),
                                          (3, exps), (-1, norm_x), (2, copy_xn2T), (0, exp_scores), (-1, copy_xnT),
                                          (-1, mask_add), (1, rough(rough_c, c_resid, RESID, rstd_c))))

            nc.scalar.preload_act_table(ACT.Silu)
            pairs = pairs_of(act)

            def silu(u):
                W = tiles(u) * P
                act.wait_ge(gu_ps, u.n + 1)
                wait(act, h_s, u.n * 3)
                if u.kind == "over":
                    a.activation(sg[:, 0, 0:P], bank[u.par][:, 0:P], ACT.Silu).then_inc(silu_s, 1)
                    a.activation(sg[:, 0, P:F], bank[u.par][:, 2 * P:2 * P + FR], ACT.Silu).then_inc(silu_s, 1)
                    return
                a.activation(sg[:, 0, 0:W], bank[u.par][:, 0:W], ACT.Silu).then_inc(silu_s, 1)
                a.activation(sg[0:FR, 1, 0:W], bank[2 + u.par][0:FR, 0:W], ACT.Silu).then_inc(silu_s, 1)

            def h_high(u):
                W = tiles(u) * P
                wait(act, y_ps, upto(u, 2))
                if u.kind == "over":
                    act.wait_ge(hT_ps, u.n - E + 1)
                    a.copy(hh[u.par][:, :, 0:P], turned(u)).then_inc(hh_s, 1)
                    return
                act.wait_ge(h_s, (u.n + 1) * 3)
                a.copy(hh[u.par][:, :, 0:W], h[:, :, 0:W]).then_inc(hh_s, 1)

            def y_out(u):
                act.wait_ge(wt_s, u.n + 1)
                wait(act, scattered, upto(u, 2) * 16)
                for t in range(tiles(u)):
                    act.wait_ge(y_ps, before(u) + t + 1)
                    a.activation(ys[u.par][:, t, :], bank[4 + t][:], ACT.Copy, scale=wt[u.par][:, t:t + 1]).then_inc(ys_s, 1)

            def x_high(u):
                wait(act, gu_ps, u.n - 1)
                for t in range(tiles(u)):
                    act.wait_ge(xT_ps, before(u) + t + 1)
                    a.copy(xh[u.par][:, :, t * P:(t + 1) * P],
                           bank[6 + t][:].rearrange("p (c t) -> p c t", c=DK)).then_inc(xh_s, 1)

            def w1_high(u):
                act.wait_ge(w1_in[u.par], (u.turn + 1) * 16)
                wait(act, gu_ps, u.n - 1)
                a.copy(w1h[u.par][:].rearrange("p c f -> p (c f)"), raw1[u.par][:]).then_inc(w1h_s, 1)

            def w2_high(u):
                act.wait_ge(w2_in[u.par], (u.turn + 1) * 32)
                wait(act, y_ps, upto(u, 2))
                a.copy(w2h[u.par][:, 0, :], raw2[u.par][:, 0, :])
                a.copy(w2h[u.par][0:FR, 1, :], raw2[u.par][0:FR, 1, :]).then_inc(w2h_s, 1)

            phase2(act, pairs, lambda s: units(s, (1, silu), (-1, w1_high), (1, h_high), (2, y_out), (-1, x_high), (0, w2_high)))

        @block.tensor
        def _(pe):
            pe.wait_ge(const_pool, CONSTS)
            pe.wait_ge(const_in, 32)

            def turn_probs(b):
                pe.wait_ge(probs_sb, b.n + 1)
                wait(pe, pT_sb, b.n)
                for c in range(MK):
                    mm = pe.transpose(bank[2][0:MC, c * T:(c + 1) * T], pr[b.par][:, c * MC:(c + 1) * MC], ident[0:T, 0:T])
                mm.then_inc(pT_ps, 1)

            def turn_xn2(b):
                pe.wait_ge(xn2_s, b.n + 1)
                wait(pe, xn2T_sb, b.n)
                for c in range(DK):
                    mm = pe.transpose(bank[4][:, c * T:(c + 1) * T], xn2[b.par][:, c * P:(c + 1) * P], ident[0:T, 0:T])
                mm.then_inc(xn2T_ps, 1)

            def scores(b):
                pe.wait_ge(ctxT_in[b.par], (b.turn + 1) * 16)
                pe.wait_ge(xnT_sb, b.n + 1)
                wait(pe, c_score, b.n * SCORE)
                for c in range(DK):
                    mm = pe.matmul(bank[1][0:T, 0:M], xnT[b.par][:, c, :], ctxT_s[b.par][:, c, :],
                                   start=(c == 0), stop=(c == DK - 1))
                mm.then_inc(score_ps, 1)

            def readout(b):
                pe.wait_ge(ctx_in[b.par], (b.turn + 1) * 16)
                pe.wait_ge(pT_sb, b.n + 1)
                wait(pe, c_resid, b.n * RESID)
                for c in range(MK):
                    mm = pe.matmul(bank[3][0:T, :], pT[b.par][:, c, :], ctx_s[b.par][:, c, :],
                                   start=(c == 0), stop=(c == MK - 1))
                mm.then_inc(read_ps, 1)

            def logits(b):
                pe.wait_ge(xn2T_sb, b.n + 1)
                wait(pe, c_top, b.n * TOP)
                for c in range(DK):
                    mm = pe.matmul(bank[5][0:T, 0:E], xn2T[b.par][:, c, :], gw_s[:, c, :],
                                   start=(c == 0), stop=(c == DK - 1))
                mm.then_inc(logit_ps, 1)

            def places(b):
                pe.wait_ge(c_top, (b.n + 1) * TOP)
                wait(pe, c_place, b.n * PLACE)
                pe.matmul(bank[6][0:T, 0:E], tri[:], mk[b.par][:, 1, :], start=True, stop=False)
                mm = pe.matmul(bank[6][0:T, 0:E], ones_b[0:T, 0:T], run[b.par][:, 1, :], start=False, stop=True)
                mm.then_inc(place_ps, 1)

            def turn_xn(b):
                pe.wait_ge(xn_s, b.n + 1)
                wait(pe, xnT_sb, b.n)
                for c in range(DK):
                    mm = pe.transpose(bank[0][:, c * T:(c + 1) * T], xn[b.par][:, c * P:(c + 1) * P], ident[0:T, 0:T])
                mm.then_inc(xnT_ps, 1)

            phase1(pe, lambda s: batches(s, (1, turn_probs), (0, scores), (1, readout), (2, turn_xn2),
                                         (-1, turn_xn), (2, logits), (3, places)))

            pe.wait_ge(c_top, B * TOP)
            pe.matmul(bank[7][0:E, 0:E], ones_b[0:T, 0:E], run[0][:, 0, :], start=True, stop=True)
            pe.matmul(bank[7][0:E, 64:80], run[0][:, 0, :], ones_b[0:T, 0:16], start=True, stop=True)
            pe.matmul(bank[7][0:E, 80:96], run[0][:, 1, :], ones_b[0:T, 0:16], start=True, stop=True).then_inc(plan_ps, 1)
            pe.wait_ge(c_plan, PLAN_A)
            pe.matmul(bank[7][:, 128:192], nover_b[:], tri_incl[:], start=True, stop=True)
            pe.matmul(bank[7][:, 192:256], nover_b[:], ident_b[:], start=True, stop=True)
            pe.matmul(bank[7][:, 256:320], map_b[:], ident_b[:], start=True, stop=True).then_inc(plan_ps, 1)

            pairs = pairs_of(pe)

            def turn_rows(u):
                pe.wait_ge(gathered[u.par], (before_par(u) + tiles(u)) * 16)
                wait(pe, xh_s, before(u))
                wait(pe, xl_s, before(u))
                for t in range(tiles(u)):
                    for c in range(DK):
                        mm = pe.transpose(bank[6 + t][:, c * P:(c + 1) * P], xg[u.par][:, t, c * P:(c + 1) * P], ident[:])
                    mm.then_inc(xT_ps, 1)

            def gate_up(u):
                W = tiles(u) * P
                pe.wait_ge(w1l_s, u.n + 1)
                pe.wait_ge(xl_s, before(u) + tiles(u))
                wait(pe, h_s, (u.n - 1) * 3)
                if u.kind == "over":
                    o = bank[u.par][:, 0:2 * F]
                    for c in range(DK):
                        wh, wl, mh, ml = w1h[u.par][:, c, :], w1l[u.par][:, c, :], xh[u.par][:, c, 0:P], xl[u.par][:, c, 0:P]
                        pe.matmul(o, mh, wh, start=(c == 0), stop=False)
                        pe.matmul(o, mh, wl, start=False, stop=False)
                        mm = pe.matmul(o, ml, wh, start=False, stop=(c == DK - 1))
                    mm.then_inc(gu_ps, 1)
                    return
                for m in range(3):
                    o = (bank[u.par][:, m * UNIT:m * UNIT + W] if m < 2 else bank[2 + u.par][:, 0:W])
                    for c in range(DK):
                        wh, wl = w1h[u.par][:, c, m * P:(m + 1) * P], w1l[u.par][:, c, m * P:(m + 1) * P]
                        mh, ml = xh[u.par][:, c, 0:W], xl[u.par][:, c, 0:W]
                        pe.matmul(o, wh, mh, start=(c == 0), stop=False)
                        pe.matmul(o, wh, ml, start=False, stop=False)
                        mm = pe.matmul(o, wl, mh, start=False, stop=(c == DK - 1))
                mm.then_inc(gu_ps, 1)

            def turn_h(u):
                pe.wait_ge(h_s, (u.n + 1) * 3)
                wait(pe, hl_s, u.n - 1)
                for k in range(2):
                    mm = pe.transpose(bank[2 + u.par][:, k * P:(k + 1) * P], h[:, 0, k * P:(k + 1) * P], ident[:])
                mm.then_inc(hT_ps, 1)

            def down(u):
                pe.wait_ge(hl_s, u.n + 1)
                pe.wait_ge(w2l_s, u.n + 1)
                wait(pe, ys_s, before(u))
                for t in range(tiles(u)):
                    s = slice(t * P, (t + 1) * P)
                    o = bank[4 + t][:]
                    pe.matmul(o, hh[u.par][:, 0, s], w2h[u.par][:, 0, :], start=True, stop=False)
                    pe.matmul(o, hh[u.par][:, 0, s], w2l[u.par][:], start=False, stop=False)
                    pe.matmul(o, hl[u.par][:, 0, s], w2h[u.par][:, 0, :], start=False, stop=False)
                    pe.matmul(o, hh[u.par][:, 1, s], w2h[u.par][:, 1, :], start=False, stop=False)
                    pe.matmul(o, hl[u.par][0:FR, 1, s], w2h[u.par][0:FR, 1, :], start=False, stop=True).then_inc(y_ps, 1)

            phase2(pe, pairs, lambda s: units(s, (-1, turn_rows), (1, only("over", turn_h)), (0, gate_up), (1, down)))


CONSTS = 15 + 3 * NSENT

PLAN_A = 20
PLAN = PLAN_A + 18


def kernel(x, ctx_2048, mask_BxS2_bk0, L0_ffn_gate_weight, L0_ffn_gate_up_proj, L0_ffn_down_proj, L0_ffn_similarity):
    import numpy as np
    import concourse.bacc as bacc
    from concourse.bass_utils import run_bass_kernel_spmd

    ctx = np.asarray(ctx_2048)
    ctxT = ctx.transpose(0, 2, 1).reshape(B, DK, P, M).transpose(0, 2, 1, 3)
    gwT = np.asarray(L0_ffn_gate_weight).T.reshape(DK, P, E).transpose(1, 0, 2)
    gu = np.asarray(L0_ffn_gate_up_proj)
    gate, up = gu[:, :F], gu[:, F:]
    w1 = np.concatenate([gate[:, :P], up[:, :P], gate[:, P:], up[:, P:]], axis=1)
    w1 = w1.transpose(0, 2, 1).reshape(E, DK, P, 2 * F).transpose(0, 2, 1, 3).reshape(E, P, DK * 2 * F)
    w2 = np.asarray(L0_ffn_down_proj).transpose(0, 2, 1)
    data = {
        "in_x": np.asarray(x), "in_ctx": ctx, "in_ctxT": ctxT,
        "in_mask": np.asarray(mask_BxS2_bk0), "in_gwT": gwT, "in_w1": w1,
        "in_w2a": w2[:, :P], "in_w2b": w2[:, P:], "in_sim": np.asarray(L0_ffn_similarity),
    }
    data = {k: np.ascontiguousarray(a) for k, a in data.items()}
    nc = bacc.Bacc("TRN2", target_bir_lowering=False, num_devices=1)
    args = [nc.dram_tensor(k, a.shape, mybir.dt.from_np(a.dtype), kind="ExternalInput").ap() for k, a in data.items()]
    args.append(nc.dram_tensor("out_rows", (ROWS, D), F32, kind="ExternalOutput").ap())
    program(nc, *args)
    rows = run_bass_kernel_spmd(nc, [data], core_ids=[0]).results[0]["out_rows"]
    return rows[:TOK].reshape(B, T, D)
```

```python
from contextlib import ExitStack

import concourse.bass as bass
from concourse import mybir

ALU = mybir.AluOpType
ACT = mybir.ActivationFunctionType
AX = mybir.AxisListType.X
F32 = mybir.dt.float32
F32R = mybir.dt.float32r
BF16 = mybir.dt.bfloat16
I32 = mybir.dt.int32
U32 = mybir.dt.uint32
U8 = mybir.dt.uint8

P = 128
B, T, D = 16, 112, 512
M, MC = 375, 125
MK = M // MC
DK = D // P
E, TOPK, SELK = 64, 8, 4
THRESH = 0.5
F = 192
FR = F - P
TOK = B * T
LIST = TOK
UNIT = 256
OVER = 128
PAD_LIST = E * LIST
ROWS = TOK + UNIT
ROW = D + E
PCOLS = 5
ENTERS = T * TOPK // P
NSENT = TOPK - SELK
MAX_OVER = 128
EPS = 1e-5
SCALE = float(D) ** -0.5
NEG = 1e30
LOW_KEY = -87.33


class At:

    def __init__(self, g, off, kind=None):
        self.g, self.off, self.kind = g, off, kind
        self.par = off % 2
        self.turn = g + off // 2 if not isinstance(g, int) or g else off // 2
        self.n = g * 2 + off if not isinstance(g, int) or g else off

    def __sub__(self, lag):
        return At(self.g, self.off - lag, self.kind)


def program(nc, x, ctx, ctxT, mask, gwT, w1, w2a, w2b, sim, out):
    table = nc.dram_tensor("list_table", (PAD_LIST + UNIT, 1), I32, kind="Internal").ap()
    normed = nc.dram_tensor("normed_tokens", (ROWS, ROW), F32, kind="Internal").ap()
    plan_d = nc.dram_tensor("plan_rows", (MAX_OVER, PCOLS), I32, kind="Internal").ap()

    with ExitStack() as stack:
        def sb(name, shape, dt=F32):
            return stack.enter_context(nc.sbuf_tensor(name, shape, dt))

        def two(name, shape, dt=F32):
            return [sb(f"{name}{i}", shape, dt) for i in range(2)]

        def rstd_tiles(name):
            return {k: sb(f"rstd_{name}_{k}", [T, 1]) for k in ("var", "log", "rough", "square", "half", "exact")}

        def sem(name):
            return stack.enter_context(nc.semaphore(name))

        def sem2(name):
            return [sem(f"{name}{i}") for i in range(2)]

        bank = [stack.enter_context(nc.psum_tensor(f"bank{i}", [P, 512], F32)) for i in range(8)]

        ident = sb("ident", [P, P])
        not_ident = sb("not_ident", [E, E])
        tri = sb("tri", [T, T], BF16)
        minus = sb("minus", [T, T], BF16)
        tri_incl = sb("tri_incl", [E, E], BF16)
        ident_b = sb("ident_b", [E, E], BF16)
        ones_b = sb("ones_b", [P, P], BF16)
        ones_f = sb("ones_f", [E, P])
        col_i = sb("col_i", [P, E], I32)
        col = sb("col", [P, E])
        list_base = sb("list_base", [P, E])
        spread_to = sb("spread_to", [T, P])
        turn_of = sb("turn_of", [T, P - T, ENTERS])
        column_is = sb("column_is", [T, ENTERS])
        over_thr = sb("over_thr", [P, 12])
        pair_thr = sb("pair_thr", [P, E])
        row_i = sb("row_i", [P, 1], I32)
        row = sb("row", [P, 1])
        zeros = sb("zeros", [P, ROW])
        blank = sb("blank", [E, LIST // UNIT, UNIT], I32)
        sim_s = sb("sim_s", [E, E])
        gw_s = sb("gw_s", [P, DK, E])

        xa = two("x_for_norm", [T, D])
        xr = two("x_for_residual", [T, D])
        ctxT_s = two("ctxT_s", [P, DK, M])
        ctx_s = two("ctx_s", [MC, MK, D])
        mask_s = two("mask_s", [T, M], U8)
        st_a = sb("st_a", [T, 6]); mv_a = sb("mv_a", [T, 2]); rstd_a = rstd_tiles("a")
        xn = two("xn", [T, D])
        xnT = two("xnT", [P, DK, T])
        madd = two("madd", [T, M])
        shift_a = sb("shift_a", [T, 1]); shift_c = sb("shift_c", [T, 1])
        sc = two("scores", [T, M])
        nmax = two("nmax", [T, 1])
        pr = two("probs", [T, M])
        rsum = two("rsum", [T, 1])
        pT = two("probsT", [MC, MK, T])
        rinv = sb("rinv", [T, 1]); rval = sb("rval", [T, 1])
        st_c = sb("st_c", [T, 6]); mv_c = sb("mv_c", [T, 2]); rstd_c = rstd_tiles("c")
        x1 = two("x1", [T, D])
        xn2 = two("xn2", [T, D])
        xn2T = two("xn2T", [P, DK, T])
        lmax = sb("lmax", [T, 1])
        key = two("key", [T, E + NSENT])
        key8 = sb("key8", [T, TOPK])
        key4 = sb("key4", [T, TOPK])
        rest = sb("rest", [T, 2, E + NSENT])
        mk = two("mk", [T, 2, E], BF16)
        run = two("run", [T, 2, E], BF16)
        eall = two("eall", [T, E])
        esum = two("esum", [T, 1])
        einv = sb("einv", [T, 1]); pm = sb("pm", [T, E]); s8 = sb("s8", [T, 1])
        s8c = sb("s8c", [T, 1]); s8i = sb("s8i", [T, 1])
        wd = two("wd", [T, E])
        placed = sb("placed", [T, E]); placed8 = sb("placed8", [T, TOPK])
        last8 = sb("last8", [T, ENTERS])
        slot8 = two("slot8", [P, ENTERS], I32)
        token = two("token", [P, ENTERS], I32)

        prim = sb("prim", [E, E]); pen = sb("pen", [E, E]); simd = sb("simd", [E, E])
        sime = sb("sime", [E, E]); cand = sb("cand", [E, E]); candm = sb("candm", [E, E])
        best = sb("best", [E, 8]); bidx = sb("bidx", [E, 8], U32); bidxf = sb("bidxf", [E, 1])
        cp = sb("cp", [E, 1]); tot = sb("tot", [E, 1]); sec = sb("sec", [E, 1])
        rep = sb("rep", [E, 1]); repl = sb("repl", [E, 1]); diff = sb("diff", [E, 1])
        mapping = sb("mapping", [E, 1])
        over_is = sb("over_is", [E, 12]); nover = sb("nover", [E, 1])
        nover_b = sb("nover_b", [E, P], BF16); map_b = sb("map_b", [E, P], BF16)
        cum = sb("cum", [P, E]); le = sb("le", [P, E]); len_ = sb("len_", [P, E])
        eid = sb("eid", [P, 1]); pre = sb("pre", [P, 1])
        ohm = sb("ohm", [P, E]); ohs = sb("ohs", [P, E])
        rel = sb("rel", [P, 1]); relv = sb("relv", [P, 1]); real = sb("real", [P, 1])
        pairs_is = sb("pairs_is", [P, E])
        planf = sb("planf", [P, PCOLS])
        plani = sb("plani", [P, PCOLS], I32)
        prow = sb("prow", [1, MAX_OVER * PCOLS], I32)

        raw1 = two("raw1_", [P, DK * 2 * F])
        raw2 = two("raw2_", [P, 2, D])
        w1h = two("w1h", [P, DK, 2 * F], F32R)
        w1l = two("w1l", [P, DK, 2 * F], F32R)
        w2h = two("w2h", [P, 2, D], F32R)
        w2l = two("w2l", [P, D], F32R)
        lg = two("list_for_gather", [P, 2], I32)
        lists = [two("list_held", [P, 2], I32), two("list_passed", [P, 2], I32)]
        ls = two("list_for_scatter", [P, 2], I32)
        xg = two("xg", [P, 2, ROW])
        wt_early = two("wt_early", [P, 2]); wt = two("wt", [P, 2])
        xh = two("xh", [P, DK, UNIT], F32R)
        xl = two("xl", [P, DK, UNIT], F32R)
        sg = sb("sg", [P, 2, UNIT])
        h = sb("h", [P, 2, UNIT])
        hh = two("hh", [P, 2, UNIT], F32R)
        hl = two("hl", [P, 2, UNIT], F32R)
        ys = two("ys", [P, 2, D])

        const_pool = sem("const_pool"); const_dve = sem("const_dve"); const_in = sem("const_in")
        filled = sem("filled")
        x_in = sem2("x_in"); xr_in = sem2("xr_in"); ctxT_in = sem2("ctxT_in"); ctx_in = sem2("ctx_in")
        mask_in = sem2("mask_in")
        x1_out = sem2("x1_out"); xn2_out = sem2("xn2_out")
        c_norm = sem("c_norm"); c_normed = sem("c_normed"); c_renorm = sem("c_renorm"); xn_s = sem("xn_s"); xn2_s = sem("xn2_s"); madd_s = sem("madd_s"); wd_out = sem2("wd_out"); wt_early_s = sem("wt_early_s"); wt_s = sem("wt_s"); c_score = sem("c_score"); c_resid = sem("c_resid")
        c_top = sem("c_top"); c_place = sem("c_place"); c_slots = sem("c_slots")
        xnT_ps = sem("xnT_ps"); score_ps = sem("score_ps"); pT_ps = sem("pT_ps"); read_ps = sem("read_ps")
        xn2T_ps = sem("xn2T_ps"); logit_ps = sem("logit_ps"); place_ps = sem("place_ps"); spread_ps = sem("spread_ps")
        xnT_sb = sem("xnT_sb"); probs_sb = sem("probs_sb"); pT_sb = sem("pT_sb"); xn2T_sb = sem("xn2T_sb")
        exps_sb = sem("exps_sb"); rough_a = sem("rough_a"); rough_c = sem("rough_c")
        tabled = sem2("tabled")
        plan_ps = sem("plan_ps"); c_plan = sem("c_plan"); plan_out = sem("plan_out"); plan_in = sem("plan_in")
        w1_in = sem2("w1_in"); w2_in = sem2("w2_in"); lg_in = sem2("lg_in");
        held_s = sem("held_s"); passed_s = sem("passed_s"); taken_s = sem("taken_s")
        gathered = sem2("gathered"); scattered = sem("scattered")
        w1h_s = sem("w1h_s"); w1l_s = sem("w1l_s"); w2h_s = sem("w2h_s"); w2l_s = sem("w2l_s")
        xT_ps = sem("xT_ps"); gu_ps = sem("gu_ps"); hT_ps = sem("hT_ps"); y_ps = sem("y_ps")
        xh_s = sem("xh_s"); xl_s = sem("xl_s"); silu_s = sem("silu_s"); h_s = sem("h_s")
        hh_s = sem("hh_s"); hl_s = sem("hl_s"); ys_s = sem("ys_s")
        linked = sem("linked"); cleared = sem("cleared"); spacer = sem("spacer")

        NORM, NORMED, SCORE, RESID, RENORM, TOP, PLACE, SLOTS = 1, 1, 1, 2, 1, 2, 2, 1

        def split_wait(eng, s, value):
            wait(eng, s, value)
            if not isinstance(value, int):
                eng.sem_inc(spacer, 1)

        def wait(eng, s, value):
            if not isinstance(value, int) or value > 0:
                eng.wait_ge(s, value)

        class Chain:
            count = 0

            def __init__(self, eng, s, told, n):
                self.eng, self.s, self.told, self.base, self.c = eng, s, told, n * told, 0

            def link(self, ins, tell=False, alone=False):
                if tell:
                    self.c += 1
                    ins.then_inc(self.s, 1)
                    yield
                    if self.c < self.told:
                        (split_wait if alone else wait)(self.eng, self.s, self.base + self.c)
                else:
                    Chain.count += 1
                    mine = Chain.count
                    ins.then_inc(linked, 1)
                    yield
                    self.eng.wait_ge(linked, mine)

            def done(self):
                assert self.c == self.told, (self.c, self.told)

            @staticmethod
            def start_again(eng):
                if Chain.count:
                    eng.wait_ge(linked, Chain.count)
                    eng.sem_clear(linked)
                Chain.count = 0

        def taking_turns(slot, *stages):
            going = []
            batches(slot, *((lag, lambda b, stage=stage: going.append(stage(b))) for lag, stage in stages))
            while going:
                going = [chain for chain in going if next(chain, "ended") != "ended"]

        def phase1(eng, body):
            for n in range(-2, 6):
                body(At(0, n))
            with eng.Fori(3, 6, 2) as g:
                for j in range(4):
                    body(At(g, j))
            for n in range(14, 21):
                body(At(0, n))

        def batches(slot, *stages):
            for lag, stage in stages:
                b = slot - lag
                if not isinstance(b.g, int) or 0 <= b.off < B:
                    stage(b)

        def phase2(eng, pairs, body):
            for n in range(-3, 4):
                body(At(0, n))
            with eng.Fori(2, 30) as g:
                for j in range(2):
                    body(At(g, j, "main"))
            for n in range(60, 68):
                body(At(0, n))
            with eng.Fori(34, pairs + 32) as g:
                for j in range(2):
                    body(At(g, j, "over"))
            for j in range(2):
                body(At(pairs + 32, j, "last"))

        def units(slot, *stages):
            for lag, stage in stages:
                u = slot - lag
                if slot.kind == "last" and u.off >= 0:
                    continue
                if slot.kind is None:
                    if u.off < 0:
                        continue
                    u.kind = "main" if u.off < E else "over"
                if u.kind == "last":
                    u.kind = "over"
                stage(u)

        def only(kind, stage):
            def do(u):
                if u.kind == kind:
                    stage(u)
            return do

        def tiles(u):
            return 2 if u.kind == "main" else 1

        def upto(u, back):
            if u.kind == "main" or (isinstance(u.g, int) and u.off - back < E):
                return (u.n - back + 1) * 2
            return u.n - back + 1 + E

        def before(u):
            return upto(u, 1)

        def before_par(u):
            return u.turn * 2 if u.kind == "main" else u.turn + E // 2

        def turned(u):
            return bank[2 + u.par][:, 0:2 * P].rearrange("p (k t) -> p k t", k=2)

        def pairs_of(eng):
            eng.wait_ge(plan_in, 16)
            return eng.value_load(prow[0:1, 3:4], min_val=3, max_val=59)

        block = stack.enter_context(nc.Block())

        @block.sync
        def _(sp):
            FILL_AT = 0
            def load_early(b):
                split_wait(sp, xn_s, b.n - 1)
                sp.dma_start(xa[b.par][:], x[bass.ds(b.n, 1)].rearrange("a t d -> (a t) d")).then_inc(x_in[b.par], 16)
                split_wait(sp, score_ps, b.n - 1)
                sp.dma_start(ctxT_s[b.par][:], ctxT[bass.ds(b.n, 1)].rearrange("a p c m -> (a p) c m")).then_inc(ctxT_in[b.par], 16)
                split_wait(sp, madd_s, b.n - 1)
                sp.dma_start(mask_s[b.par][:], mask[bass.ds(b.n, 1)].broadcast_to([T, M])).then_inc(mask_in[b.par], 16)

            def load_late(b):
                split_wait(sp, read_ps, b.n - 1)
                sp.dma_start(ctx_s[b.par][:], ctx[bass.ds(b.n, 1)].rearrange("a (c p) d -> (a p) c d", p=MC)).then_inc(ctx_in[b.par], 16)
                split_wait(sp, c_resid, (b.n - 1) * RESID)
                sp.dma_start(xr[b.par][:], x[bass.ds(b.n, 1)].rearrange("a t d -> (a t) d")).then_inc(xr_in[b.par], 16)

            def store(b):
                split_wait(sp, c_resid, b.n * RESID + 1)
                sp.dma_start(out[bass.ds(b.n * T, T), :], x1[b.par][:]).then_inc(x1_out[b.par], 16)

            def store_normed(b):
                split_wait(sp, xn2_s, b.n + 1)
                sp.dma_start(normed[bass.ds(b.n * T, T), 0:D], xn2[b.par][:]).then_inc(xn2_out[b.par], 16)

            def store_weights(b):
                split_wait(sp, c_place, b.n * PLACE + 1)
                sp.dma_start(normed[bass.ds(b.n * T, T), D:ROW], wd[b.par][:]).then_inc(wd_out[b.par], 16)

            def fill(b):
                sp.wait_ge(const_pool, 2)
                sp.dma_start(out[TOK:TOK + P, :], zeros[:, 0:D]).then_inc(filled, 16)
                sp.dma_start(out[TOK + P:ROWS, :], zeros[:, 0:D]).then_inc(filled, 16)
                sp.dma_start(normed[TOK:TOK + P, :], zeros[:]).then_inc(filled, 16)
                sp.dma_start(normed[TOK + P:ROWS, :], zeros[:]).then_inc(filled, 16)
                sp.wait_ge(const_pool, 3)
                sp.dma_start(table[0:PAD_LIST].rearrange("(e n) c -> e (n c)", e=E),
                             blank[:].rearrange("e a b -> e (a b)")).then_inc(filled, 16)
                sp.dma_start(table[PAD_LIST:PAD_LIST + UNIT].rearrange("(o n) c -> o (n c)", o=1),
                             blank[0:1, 0]).then_inc(filled, 16)

            def slot(s):
                batches(s, (-2, load_early), (-1, load_late))
                if isinstance(s.g, int) and s.off == -2:
                    sp.dma_start(gw_s[:], gwT).then_inc(const_in, 16)
                    sp.dma_start(sim_s[:], sim).then_inc(const_in, 16)
                if isinstance(s.g, int) and s.off == FILL_AT:
                    fill(s)
                batches(s, (2, store_normed), (4, store_weights), (1, store))

            phase1(sp, slot)

            sp.wait_ge(c_plan, PLAN)
            sp.dma_start(plan_d, plani[:]).then_inc(plan_out, 16)
            sp.wait_ge(plan_out, 16)
            sp.dma_start(prow[:], plan_d.rearrange("(o r) c -> o (r c)", o=1)).then_inc(plan_in, 16)
            pairs = pairs_of(sp)
            def expert(u):
                if u.kind == "main":
                    return sp.value_load(prow[0:1, bass.ds(u.n * PCOLS + 2, 1)], min_val=0, max_val=E - 1)
                return sp.value_load(prow[0:1, bass.ds((u.n - E) * PCOLS, 1)], min_val=0, max_val=E - 1)

            def first_entry(u):
                if u.kind == "main":
                    return u.n * LIST
                return sp.value_load(prow[0:1, bass.ds((u.n - E) * PCOLS + 1, 1)], min_val=0, max_val=PAD_LIST)

            def load_list(u, dst, s):
                n = tiles(u)
                rows = table[bass.ds(first_entry(u), n * P), :].rearrange("(p t) c -> p (t c)", p=P)
                sp.dma_start(dst[u.par][:, 0:n], rows).then_inc(s[u.par], 16)

            def load_w1(u):
                split_wait(sp, w1h_s, u.n - 1)
                split_wait(sp, w1l_s, u.n - 1)
                sp.dma_start(raw1[u.par][:], w1[bass.ds(expert(u), 1)].rearrange("a p f -> (a p) f")).then_inc(w1_in[u.par], 16)

            def load_w2(u):
                split_wait(sp, w2h_s, u.n - 1)
                split_wait(sp, w2l_s, u.n - 1)
                e = expert(u)
                sp.dma_start(raw2[u.par][:, 0, :], w2a[bass.ds(e, 1)].rearrange("a p f -> (a p) f")).then_inc(w2_in[u.par], 16)
                sp.dma_start(raw2[u.par][0:FR, 1, :], w2b[bass.ds(e, 1)].rearrange("a p f -> (a p) f")).then_inc(w2_in[u.par], 16)

            def load_for_gather(u):
                split_wait(sp, gathered[u.par], before_par(u) * 16)
                split_wait(sp, held_s, u.n - 1)
                load_list(u, lg, lg_in)

            for n in range(2):
                load_w1(At(0, n, "main"))
            for p in range(2):
                sp.wait_ge(tabled[p], B // 2 * ENTERS * 16)

            def later(n, stage):
                def do(u):
                    if not isinstance(u.n, int) or u.n >= n:
                        stage(u)
                return do

            def slot2(s):
                units(s, (-2, later(2, load_w1)), (-3, load_for_gather), (-1, later(1, load_w2)))
                if isinstance(s.g, int) and s.off == -2:
                    load_w2(At(0, 0, "main"))

            phase2(sp, pairs, slot2)
            n = pairs * 2 + E
            split_wait(sp, scattered, (pairs * 2 + 2 * E) * 16)
            for p in range(2):
                split_wait(sp, w1_in[p], (pairs + E // 2 + 1) * 16)
                split_wait(sp, gathered[p], (pairs + E // 2 + 1 + E // 2) * 16)
            split_wait(sp, w2_in[0], (pairs + E // 2 + 1) * 32)
            split_wait(sp, lg_in[0], (pairs + E // 2 + 2 - 1) * 16)
            split_wait(sp, lg_in[1], (pairs + E // 2 + 1) * 16)
            split_wait(sp, lg_in[0], (pairs + E // 2 + 2) * 16)

        @block.gpsimd
        def _(pool):
            nc.gpsimd.memset(ident[:], 0.0).then_inc(cleared, 1)
            pool.wait_ge(cleared, 1)
            nc.gpsimd.affine_select(out=ident[:], in_=ident[:], compare_op=ALU.not_equal, fill=1.0, base=0,
                                    pattern=[[-1, P]], channel_multiplier=1).then_inc(const_pool, 1)
            nc.gpsimd.memset(zeros[:], 0.0).then_inc(const_pool, 1)
            nc.gpsimd.iota(blank[:], [[0, LIST // UNIT], [1, UNIT]], base=TOK,
                           channel_multiplier=0).then_inc(const_pool, 1)
            nc.gpsimd.memset(tri[:], -1.0).then_inc(cleared, 1)
            nc.gpsimd.memset(tri_incl[:], 1.0).then_inc(cleared, 1)
            nc.gpsimd.memset(ident_b[:], 0.0).then_inc(cleared, 1)
            nc.gpsimd.memset(spread_to[:], 1.0).then_inc(cleared, 1)
            nc.gpsimd.memset(turn_of[:], 0.0).then_inc(cleared, 1)
            pool.wait_ge(cleared, 6)
            nc.gpsimd.affine_select(out=tri[:], in_=tri[:], compare_op=ALU.is_gt, fill=0.0, base=0,
                                    pattern=[[1, T]], channel_multiplier=-1).then_inc(const_pool, 1)
            nc.gpsimd.affine_select(out=tri_incl[:], in_=tri_incl[:], compare_op=ALU.is_ge, fill=0.0, base=0,
                                    pattern=[[1, E]], channel_multiplier=-1).then_inc(const_pool, 1)
            nc.gpsimd.affine_select(out=ident_b[:], in_=ident_b[:], compare_op=ALU.not_equal, fill=1.0, base=0,
                                    pattern=[[-1, E]], channel_multiplier=1).then_inc(const_pool, 1)
            nc.gpsimd.memset(ones_b[:], 1.0).then_inc(const_pool, 1)
            nc.gpsimd.memset(minus[:], -1.0).then_inc(const_pool, 1)
            nc.gpsimd.memset(ones_f[:], 1.0).then_inc(const_pool, 1)
            nc.gpsimd.iota(col_i[:], [[1, E]], base=0, channel_multiplier=0).then_inc(const_pool, 1)
            nc.gpsimd.iota(row_i[:], [[0, 1]], base=0, channel_multiplier=1).then_inc(const_pool, 1)
            nc.gpsimd.affine_select(out=spread_to[:], in_=spread_to[:], compare_op=ALU.is_ge, fill=0.0, base=T * ENTERS,
                                    pattern=[[-ENTERS, P]], channel_multiplier=1).then_inc(cleared, 1)
            nc.gpsimd.affine_select(out=turn_of[:], in_=turn_of[:], compare_op=ALU.not_equal, fill=1.0, base=0,
                                    pattern=[[-ENTERS, P - T], [-1, ENTERS]], channel_multiplier=1).then_inc(const_pool, 1)
            for p in range(2):
                nc.gpsimd.iota(token[p][:], [[1, ENTERS]], base=T * (p - 2) - T * ENTERS,
                               channel_multiplier=ENTERS).then_inc(cleared, 1)
            pool.wait_ge(cleared, 9)
            nc.gpsimd.affine_select(out=spread_to[:], in_=spread_to[:], compare_op=ALU.is_ge, fill=0.0,
                                    base=-T * ENTERS + ENTERS - 1, pattern=[[ENTERS, P]], channel_multiplier=-1
                                    ).then_inc(const_pool, 1)
            for p in range(2):
                nc.gpsimd.iota(token[p][0:T, :], [[0, ENTERS]], base=T * (p - 2), channel_multiplier=1).then_inc(const_pool, 1)
                for i in range(NSENT):
                    nc.gpsimd.memset(key[p][:, E + i:E + i + 1], float(i + 1)).then_inc(const_pool, 1)
            for i in range(NSENT):
                nc.gpsimd.memset(key4[:, SELK + i:SELK + i + 1], float(i + 1)).then_inc(const_pool, 1)
            nc.gpsimd.memset(planf[:], 0.0).then_inc(const_pool, 1)
            nc.gpsimd.memset(run[0][:], 0.0).then_inc(const_pool, 1)
            nc.gpsimd.memset(sg[:], 0.0).then_inc(const_pool, 1)

            pool.wait_ge(filled, 6 * 16)

            def enter(b):
                split_wait(pool, c_slots, (b.n + 1) * SLOTS)
                for k in range(ENTERS):
                    pool.indirect_dma_start(table, bass.IndirectOffsetOnAxis(ap=slot8[b.par][:, k:k + 1], axis=0),
                                            token[b.par][:, k:k + 1], None).then_inc(tabled[b.par], 16)

            phase1(pool, lambda s: batches(s, (4, enter)))

            pairs = pairs_of(pool)
            for p in range(2):
                pool.wait_ge(xn2_out[p], B // 2 * 16)
                pool.wait_ge(wd_out[p], B // 2 * 16)
                pool.wait_ge(x1_out[p], B // 2 * 16)

            def gather(u):
                split_wait(pool, lg_in[u.par], (u.turn + 1) * 16)
                split_wait(pool, xT_ps, upto(u, 2))
                split_wait(pool, wt_early_s, upto(u, 2))
                split_wait(pool, passed_s, u.n - 1)
                n = tiles(u)
                nc.gpsimd.tensor_copy(lists[0][u.par][:, 0:n], lg[u.par][:, 0:n]).then_inc(held_s, 1)
                for t in range(tiles(u)):
                    pool.indirect_dma_start(xg[u.par][:, t, :], None, normed,
                                            bass.IndirectOffsetOnAxis(ap=lg[u.par][:, t:t + 1], axis=0)
                                            ).then_inc(gathered[u.par], 16)

            def weights_early(u):
                split_wait(pool, gathered[u.par], (before_par(u) + tiles(u)) * 16)
                split_wait(pool, wt_s, u.n - 1)
                if u.kind == "main":
                    e = u.n
                else:
                    e = pool.value_load(prow[0:1, bass.ds((u.n - E) * PCOLS + 4, 1)], min_val=0, max_val=E - 1)
                n = tiles(u)
                nc.gpsimd.tensor_copy(wt_early[u.par][:, 0:n], xg[u.par][:, 0:n, bass.ds(e + D, 1)].rearrange("p t o -> p (t o)")
                                      ).then_inc(wt_early_s, n)

            def hand_list(u):
                split_wait(pool, held_s, u.n + 1)
                split_wait(pool, taken_s, u.n - 1)
                n = tiles(u)
                nc.gpsimd.tensor_copy(lists[1][u.par][:, 0:n], lists[0][u.par][:, 0:n]).then_inc(passed_s, 1)

            def take_list(u):
                split_wait(pool, passed_s, u.n + 1)
                split_wait(pool, scattered, upto(u, 2) * 16)
                n = tiles(u)
                nc.gpsimd.tensor_copy(ls[u.par][:, 0:n], lists[1][u.par][:, 0:n]).then_inc(taken_s, 1)

            def scatter(u):
                split_wait(pool, taken_s, u.n + 1)
                split_wait(pool, ys_s, before(u) + tiles(u))
                split_wait(pool, scattered, before(u) * 16)
                for t in range(tiles(u)):
                    pool.indirect_dma_start(out, bass.IndirectOffsetOnAxis(ap=ls[u.par][:, t:t + 1], axis=0),
                                            ys[u.par][:, t, :], None, compute_op=ALU.add).then_inc(scattered, 16)

            phase2(pool, pairs, lambda s: units(s, (2, take_list), (0, hand_list), (0, weights_early), (-2, gather), (2, scatter)))

        @block.vector
        def _(dve):
            v = nc.vector
            def norm(b):
                ch = Chain(dve, c_norm, NORM, b.n)
                dve.wait_ge(x_in[b.par], (b.turn + 1) * 16)
                wait(dve, xn_s, b.n)
                yield from ch.link(v.bn_stats(st_a[:], xa[b.par][:]))
                yield from ch.link(v.bn_aggr(mv_a[:], st_a[:]))
                yield from ch.link(v.tensor_scalar(rstd_a["var"][:], mv_a[:, 1:2], EPS, None, ALU.add), tell=True)
                ch.done()

            def newton(ch, r):
                yield from ch.link(v.tensor_tensor(r["square"][:], r["rough"][:], r["rough"][:], ALU.mult))
                yield from ch.link(v.tensor_scalar(r["half"][:], r["square"][:], r["var"][:], -0.5, ALU.mult, ALU.mult))
                yield from ch.link(v.scalar_tensor_tensor(r["exact"][:], r["half"][:], 1.5, r["rough"][:], ALU.add, ALU.mult))

            def normed_x(b):
                ch = Chain(dve, c_normed, NORMED, b.n)
                dve.wait_ge(rough_a, (b.n + 1) * 2)
                yield from newton(ch, rstd_a)
                yield from ch.link(v.tensor_scalar(shift_a[:], mv_a[:, 0:1], -1.0, rstd_a["exact"][:], ALU.mult, ALU.mult), tell=True)
                ch.done()

            def norm_and_scale(b):
                yield from norm(b)
                yield from normed_x(b)

            def score(b):
                ch = Chain(dve, c_score, SCORE, b.n)
                dve.wait_ge(madd_s, b.n + 1)
                dve.wait_ge(score_ps, b.n + 1)
                wait(dve, probs_sb, b.n - 1)
                wait(dve, c_resid, (b.n - 1) * RESID)
                yield from ch.link(v.scalar_tensor_tensor(sc[b.par][:], bank[1][0:T, 0:M], SCALE, madd[b.par][:], ALU.mult, ALU.add))
                yield from ch.link(v.tensor_reduce(nmax[b.par][:], sc[b.par][:], AX, ALU.max, negate=True), tell=True)
                ch.done()

            def resid(b):
                ch = Chain(dve, c_resid, RESID, b.n)
                dve.wait_ge(probs_sb, b.n + 1)
                yield from ch.link(v.reciprocal(rinv[:], rsum[b.par][:]))
                yield from ch.link(v.tensor_scalar(rval[:], nmax[b.par][:], NEG / 2, rinv[:], ALU.is_lt, ALU.mult))
                dve.wait_ge(xr_in[b.par], (b.turn + 1) * 16)
                dve.wait_ge(read_ps, b.n + 1)
                wait(dve, x1_out[b.par], b.turn * 16)
                wait(dve, xn2_s, b.n - 1)
                yield from ch.link(v.scalar_tensor_tensor(x1[b.par][:], bank[3][0:T, :], rval[:], xr[b.par][:], ALU.mult, ALU.add), tell=True, alone=True)
                yield from ch.link(v.bn_stats(st_c[:], x1[b.par][:]))
                yield from ch.link(v.bn_aggr(mv_c[:], st_c[:]))
                yield from ch.link(v.tensor_scalar(rstd_c["var"][:], mv_c[:, 1:2], EPS, None, ALU.add), tell=True)
                ch.done()

            def renormed_x(b):
                ch = Chain(dve, c_renorm, RENORM, b.n)
                dve.wait_ge(rough_c, (b.n + 1) * 2)
                wait(dve, xn2_s, b.n)
                yield from newton(ch, rstd_c)
                yield from ch.link(v.tensor_scalar(shift_c[:], mv_c[:, 0:1], -1.0, rstd_c["exact"][:], ALU.mult, ALU.mult), tell=True)
                ch.done()

            def top(b):
                ch = Chain(dve, c_top, TOP, b.n)
                dve.wait_ge(logit_ps, b.n + 1)
                yield from ch.link(v.tensor_reduce(lmax[:], bank[5][0:T, 0:E], AX, ALU.max))
                wait(dve, exps_sb, b.n - 1)
                k = key[b.par]
                yield from ch.link(v.tensor_scalar(k[:, 0:E], bank[5][0:T, 0:E], lmax[:], LOW_KEY, ALU.subtract, ALU.max), tell=True, alone=True)
                yield from ch.link(v.max(key8[:], k[:, 0:E]))
                yield from ch.link(v.tensor_copy(key4[:, 0:SELK], key8[:, 0:SELK]))
                yield from ch.link(v.match_replace(rest[:, 1, 0:E], key8[:], k[:, 0:E], 5.0))
                yield from ch.link(v.match_replace(rest[:, 0, :], key4[:], k[:], 5.0))
                wait(dve, place_ps, b.n - 1)
                wait(dve, c_place, (b.n - 1) * PLACE)
                yield from ch.link(v.tensor_scalar(mk[b.par][:], rest[:, :, 0:E], 4.5, None, ALU.is_gt))
                wait(dve, place_ps, b.n)
                yield from ch.link(v.tensor_tensor(run[1 - b.par][:], run[b.par][:], mk[b.par][:], ALU.add), tell=True)
                ch.done()

            def place_entries(b):
                ch = Chain(dve, c_place, PLACE, b.n)
                dve.wait_ge(exps_sb, b.n + 1)
                yield from ch.link(v.reciprocal(einv[:], esum[b.par][:]))
                yield from ch.link(v.scalar_tensor_tensor(pm[:], eall[b.par][:], einv[:], mk[b.par][:, 1, :], ALU.mult, ALU.mult))
                yield from ch.link(v.tensor_reduce(s8[:], pm[:], AX, ALU.add))
                yield from ch.link(v.tensor_scalar(s8c[:], s8[:], 1e-12, None, ALU.max))
                yield from ch.link(v.reciprocal(s8i[:], s8c[:]))
                wait(dve, wd_out[b.par], b.turn * 16)
                yield from ch.link(v.tensor_scalar(wd[b.par][:], pm[:], s8i[:], None, ALU.mult), tell=True)
                dve.wait_ge(place_ps, b.n + 1)
                wait(dve, spread_ps, b.n)
                yield from ch.link(v.tensor_tensor(placed[:], bank[6][0:T, 0:E], mk[b.par][:, 1, :], ALU.mult))
                yield from ch.link(v.max(placed8[:], placed[:]))
                yield from ch.link(v.tensor_scalar(last8[:], column_is[:], placed8[:, TOPK - 1:TOPK], None, ALU.mult), tell=True)
                ch.done()

            def publish(b):
                ch = Chain(dve, c_slots, SLOTS, b.n)
                dve.wait_ge(spread_ps, b.n + 1)
                wait(dve, tabled[b.par], b.turn * ENTERS * 16)
                yield from ch.link(v.tensor_scalar(slot8[b.par][:], bank[7][:, 0:ENTERS], -1.0, float(PAD_LIST), ALU.mult, ALU.add))
                yield from ch.link(v.tensor_scalar(token[b.par][:], token[b.par][:], 2 * T, None, ALU.add), tell=True)
                ch.done()

            def constants():
                dve.wait_ge(const_pool, CONSTS)
                v.tensor_copy(col[:], col_i[:]).then_inc(const_dve, 1)
                v.tensor_copy(row[:], row_i[:]).then_inc(const_dve, 1)
                v.tensor_scalar(not_ident[:], ident[0:E, 0:E], -1.0, 1.0, ALU.mult, ALU.add).then_inc(const_dve, 1)
                v.tensor_reduce(column_is[:], turn_of[:].rearrange("t p c -> t c p"), AX, ALU.add).then_inc(const_dve, 1)
                dve.wait_ge(const_dve, 4)
                v.tensor_scalar(list_base[:], col[:], -float(LIST), float(PAD_LIST), ALU.mult, ALU.add).then_inc(const_dve, 1)
                v.tensor_scalar(over_thr[:], col[:, 0:12], float(OVER), float(UNIT), ALU.mult, ALU.add).then_inc(const_dve, 1)
                v.tensor_scalar(pair_thr[:], col[:], 2.0, 6.0, ALU.mult, ALU.add).then_inc(const_dve, 1)
                dve.wait_ge(const_dve, DVE_CONSTS)

            def slot(s):
                Chain.start_again(dve)
                taking_turns(s, (4, place_entries), (3, top), (-1, norm_and_scale), (2, renormed_x))
                taking_turns(s, (0, score))
                if isinstance(s.g, int) and s.off == -1:
                    constants()
                taking_turns(s, (1, resid))
                if not (isinstance(s.n, int) and s.n == B - 1 + 4):
                    taking_turns(s, (4, publish))

            phase1(dve, slot)

            ch = Chain(dve, c_plan, PLAN, 0)

            def step(ins, tell=False):
                for _ in ch.link(ins, tell):
                    pass

            dve.wait_ge(const_in, 32)
            dve.wait_ge(plan_ps, 1)
            step(v.tensor_scalar(prim[:], bank[0][0:E, 0:E], 0.0, None, ALU.is_gt))
            step(v.tensor_copy(cp[:], bank[0][0:E, 64:65]))
            step(v.tensor_copy(tot[:], bank[0][0:E, 80:81]))
            step(v.tensor_tensor(simd[:], sim_s[:], not_ident[:], ALU.mult))
            step(v.tensor_tensor(sime[:], simd[:], ident[0:E, 0:E], ALU.add))
            step(v.tensor_tensor(candm[:], sime[:], prim[:], ALU.mult))
            step(v.tensor_scalar(pen[:], prim[:], -1.0, NEG, ALU.add, ALU.mult))
            step(v.tensor_tensor(cand[:], candm[:], pen[:], ALU.add))
            step(v.max(best[:], cand[:]))
            step(v.max_index(bidx[:], best[:], cand[:]))
            step(v.tensor_copy(bidxf[:], bidx[:, 0:1]))
            step(v.tensor_tensor(sec[:], tot[:], cp[:], ALU.is_gt))
            step(v.tensor_scalar(rep[:], cp[:], 0.0, sec[:], ALU.is_le, ALU.mult))
            step(v.tensor_scalar(repl[:], best[:, 0:1], THRESH, rep[:], ALU.is_ge, ALU.mult))
            step(v.tensor_tensor(diff[:], bidxf[:], row[0:E], ALU.subtract))
            step(v.scalar_tensor_tensor(mapping[:], diff[:], repl[:], row[0:E], ALU.mult, ALU.add))
            step(v.tensor_scalar(over_is[:], over_thr[0:E, :], tot[:], None, ALU.is_lt))
            step(v.tensor_reduce(nover[:], over_is[:], AX, ALU.add))
            step(v.tensor_scalar(nover_b[:], ones_f[:], nover[:], None, ALU.mult))
            step(v.tensor_scalar(map_b[:], ones_f[:], mapping[:], None, ALU.mult), tell=True)
            for _ in publish(At(0, B - 1)):
                pass
            dve.wait_ge(plan_ps, 2)
            step(v.tensor_scalar(le[:], bank[0][:, 128:192], row[:], None, ALU.is_le))
            step(v.tensor_reduce(eid[:], le[:], AX, ALU.add))
            step(v.tensor_tensor(len_[:], bank[0][:, 192:256], le[:], ALU.mult))
            step(v.tensor_reduce(pre[:], len_[:], AX, ALU.add))
            step(v.tensor_scalar(ohs[:], col[:], eid[:], None, ALU.is_equal))
            step(v.tensor_tensor(ohm[:], bank[0][:, 256:320], ohs[:], ALU.mult))
            step(v.tensor_reduce(planf[:, 0:1], ohm[:], AX, ALU.add))
            step(v.tensor_tensor(rel[:], row[:], pre[:], ALU.subtract))
            step(v.tensor_scalar(relv[:], rel[:], float(OVER), float(UNIT), ALU.mult, ALU.add))
            step(v.tensor_scalar(real[:], eid[:], float(E), relv[:], ALU.is_lt, ALU.mult))
            step(v.scalar_tensor_tensor(planf[:, 1:2], eid[:], float(LIST), real[:], ALU.mult, ALU.add))
            step(v.tensor_copy(planf[0:E, 2:3], mapping[:]))
            step(v.tensor_copy(cum[:], bank[0][:, 128:192]))
            step(v.tensor_scalar(pairs_is[:], pair_thr[:], cum[:, E - 1:E], None, ALU.is_lt))
            step(v.tensor_reduce(pre[:], pairs_is[:], AX, ALU.add))
            step(v.tensor_scalar(planf[:, 3:4], pre[:], 3.0, None, ALU.add))
            step(v.tensor_scalar(planf[:, 4:5], eid[:], float(E - 1), None, ALU.min))
            step(v.tensor_copy(plani[:], planf[:]), tell=True)
            ch.done()

            pairs = pairs_of(dve)

            def h_products(u):
                W = tiles(u) * P
                dve.wait_ge(silu_s, (u.n + 1) * 2)
                dve.wait_ge(gu_ps, u.n + 1)
                wait(dve, hh_s, u.n)
                wait(dve, hl_s, u.n)
                ab, c = bank[u.par], bank[2 + u.par]
                if u.kind == "over":
                    last = slice(2 * P + FR, 2 * P + 2 * FR)
                    v.tensor_tensor(h[:, 0, 0:P], sg[:, 0, 0:P], ab[:, P:2 * P], ALU.mult).then_inc(h_s, 1)
                    v.tensor_tensor(h[:, 0, P:F], sg[:, 0, P:F], ab[:, last], ALU.mult).then_inc(h_s, 1)
                    v.tensor_tensor(h[:, 0, F:2 * P], sg[:, 0, P:F], ab[:, last], ALU.mult).then_inc(h_s, 1)
                    return
                v.tensor_tensor(h[:, 0, 0:W], sg[:, 0, 0:W], ab[:, UNIT:UNIT + W], ALU.mult).then_inc(h_s, 1)
                v.tensor_tensor(h[0:FR, 1, 0:W], sg[0:FR, 1, 0:W], c[FR:P, 0:W], ALU.mult).then_inc(h_s, 1)
                v.tensor_tensor(h[FR:P, 1, 0:W], sg[0:FR, 1, 0:W], c[FR:P, 0:W], ALU.mult).then_inc(h_s, 1)

            def h_low(u):
                W = tiles(u) * P
                dve.wait_ge(hh_s, u.n + 1)
                wait(dve, y_ps, upto(u, 2))
                src = turned(u) if u.kind == "over" else h[:, :, 0:W]
                v.tensor_tensor(hl[u.par][:, :, 0:W], src, hh[u.par][:, :, 0:W].bitcast(F32),
                                ALU.subtract).then_inc(hl_s, 1)

            def x_low(u):
                wait(dve, gu_ps, u.n - 1)
                for t in range(tiles(u)):
                    dve.wait_ge(xh_s, before(u) + t + 1)
                    v.tensor_tensor(xl[u.par][:, :, t * P:(t + 1) * P], bank[6 + t][:].rearrange("p (c t) -> p c t", c=DK),
                                    xh[u.par][:, :, t * P:(t + 1) * P].bitcast(F32), ALU.subtract).then_inc(xl_s, 1)

            def w1_low(u):
                dve.wait_ge(w1h_s, u.n + 1)
                wait(dve, gu_ps, u.n - 1)
                v.tensor_tensor(w1l[u.par][:].rearrange("p c f -> p (c f)"), raw1[u.par][:],
                                w1h[u.par][:].rearrange("p c f -> p (c f)").bitcast(F32), ALU.subtract).then_inc(w1l_s, 1)

            def w2_low(u):
                dve.wait_ge(w2h_s, u.n + 1)
                wait(dve, y_ps, upto(u, 2))
                v.tensor_tensor(w2l[u.par][:], raw2[u.par][:, 0, :], w2h[u.par][:, 0, :].bitcast(F32), ALU.subtract)
                v.tensor_tensor(w2h[u.par][FR:P, 1, :], raw2[u.par][0:FR, 1, :], w2h[u.par][0:FR, 1, :].bitcast(F32),
                                ALU.subtract).then_inc(w2l_s, 1)

            def weights(u):
                wait(dve, wt_early_s, before(u) + tiles(u))
                wait(dve, ys_s, upto(u, 2))
                v.tensor_copy(wt[u.par][:, 0:tiles(u)], wt_early[u.par][:, 0:tiles(u)]).then_inc(wt_s, 1)

            phase2(dve, pairs, lambda s: units(
                s, (1, weights), (1, h_products), (1, only("over", w2_low)), (1, only("over", h_low)), (-1, w1_low),
                (1, only("main", h_low)), (-1, x_low), (0, only("main", w2_low))))

        @block.scalar
        def _(act):
            a = nc.scalar

            def copy_pT(b):
                act.wait_ge(pT_ps, b.n + 1)
                wait(act, read_ps, b.n - 1)
                a.copy(pT[b.par][:], bank[2][0:MC, 0:MK * T].rearrange("p (c t) -> p c t", c=MK)).then_inc(pT_sb, 1)

            def copy_xn2T(b):
                act.wait_ge(xn2T_ps, b.n + 1)
                wait(act, logit_ps, b.n - 1)
                a.copy(xn2T[b.par][:], bank[4][:, 0:DK * T].rearrange("p (c t) -> p c t", c=DK)).then_inc(xn2T_sb, 1)

            def exps(b):
                act.wait_ge(c_top, b.n * TOP + 1)
                wait(act, c_place, (b.n - 1) * PLACE)
                a.activation(eall[b.par][:], key[b.par][:, 0:E], ACT.Exp, accum_out=esum[b.par][:]).then_inc(exps_sb, 1)

            def mask_add(b):
                act.wait_ge(mask_in[b.par], (b.turn + 1) * 16)
                wait(act, c_score, (b.n - 1) * SCORE)
                a.activation(madd[b.par][:], mask_s[b.par][:], ACT.Copy, scale=NEG, bias=-NEG).then_inc(madd_s, 1)

            def norm_x(b):
                act.wait_ge(c_normed, (b.n + 1) * NORMED)
                wait(act, xnT_ps, b.n - 1)
                a.activation(xn[b.par][:], xa[b.par][:], ACT.Identity, bias=shift_a[:], scale=rstd_a["exact"][:]).then_inc(xn_s, 1)

            def norm_x1(b):
                act.wait_ge(c_renorm, (b.n + 1) * RENORM)
                wait(act, xn2T_ps, b.n - 1)
                wait(act, xn2_out[b.par], b.turn * 16)
                a.activation(xn2[b.par][:], x1[b.par][:], ACT.Identity, bias=shift_c[:], scale=rstd_c["exact"][:]).then_inc(xn2_s, 1)

            def exp_scores(b):
                act.wait_ge(c_score, (b.n + 1) * SCORE)
                wait(act, c_resid, (b.n - 1) * RESID)
                wait(act, pT_ps, b.n - 1)
                a.activation(pr[b.par][:], sc[b.par][:], ACT.Exp, bias=nmax[b.par][:],
                             accum_out=rsum[b.par][:]).then_inc(probs_sb, 1)

            def copy_xnT(b):
                act.wait_ge(xnT_ps, b.n + 1)
                wait(act, score_ps, b.n - 1)
                a.copy(xnT[b.par][:], bank[0][:, 0:DK * T].rearrange("p (c t) -> p c t", c=DK)).then_inc(xnT_sb, 1)

            def rough(s, c, links, r):
                def stage(b):
                    act.wait_ge(c, (b.n + 1) * links)
                    a.activation(r["log"][:], r["var"][:], ACT.Ln).then_inc(s, 1)
                    act.wait_ge(s, b.n * 2 + 1)
                    a.activation(r["rough"][:], r["log"][:], ACT.Exp, scale=-0.5).then_inc(s, 1)
                return stage

            nc.scalar.preload_act_table_set("natural_log_exp_and_others")
            phase1(act, lambda s: batches(s, (1, copy_pT), (-1, rough(rough_a, c_norm, NORM, rstd_a)), (2, norm_x1),
                                          (3, exps), (-1, norm_x), (2, copy_xn2T), (0, exp_scores), (-1, copy_xnT),
                                          (-1, mask_add), (1, rough(rough_c, c_resid, RESID, rstd_c))))

            nc.scalar.preload_act_table(ACT.Silu)
            pairs = pairs_of(act)

            def silu(u):
                W = tiles(u) * P
                act.wait_ge(gu_ps, u.n + 1)
                wait(act, h_s, u.n * 3)
                if u.kind == "over":
                    a.activation(sg[:, 0, 0:P], bank[u.par][:, 0:P], ACT.Silu).then_inc(silu_s, 1)
                    a.activation(sg[:, 0, P:F], bank[u.par][:, 2 * P:2 * P + FR], ACT.Silu).then_inc(silu_s, 1)
                    return
                a.activation(sg[:, 0, 0:W], bank[u.par][:, 0:W], ACT.Silu).then_inc(silu_s, 1)
                a.activation(sg[0:FR, 1, 0:W], bank[2 + u.par][0:FR, 0:W], ACT.Silu).then_inc(silu_s, 1)

            def h_high(u):
                W = tiles(u) * P
                wait(act, y_ps, upto(u, 2))
                if u.kind == "over":
                    act.wait_ge(hT_ps, u.n - E + 1)
                    a.copy(hh[u.par][:, :, 0:P], turned(u)).then_inc(hh_s, 1)
                    return
                act.wait_ge(h_s, (u.n + 1) * 3)
                a.copy(hh[u.par][:, :, 0:W], h[:, :, 0:W]).then_inc(hh_s, 1)

            def y_out(u):
                act.wait_ge(wt_s, u.n + 1)
                wait(act, scattered, upto(u, 2) * 16)
                for t in range(tiles(u)):
                    act.wait_ge(y_ps, before(u) + t + 1)
                    a.activation(ys[u.par][:, t, :], bank[4 + t][:], ACT.Copy, scale=wt[u.par][:, t:t + 1]).then_inc(ys_s, 1)

            def x_high(u):
                wait(act, gu_ps, u.n - 1)
                for t in range(tiles(u)):
                    act.wait_ge(xT_ps, before(u) + t + 1)
                    a.copy(xh[u.par][:, :, t * P:(t + 1) * P],
                           bank[6 + t][:].rearrange("p (c t) -> p c t", c=DK)).then_inc(xh_s, 1)

            def w1_high(u):
                act.wait_ge(w1_in[u.par], (u.turn + 1) * 16)
                wait(act, gu_ps, u.n - 1)
                a.copy(w1h[u.par][:].rearrange("p c f -> p (c f)"), raw1[u.par][:]).then_inc(w1h_s, 1)

            def w2_high(u):
                act.wait_ge(w2_in[u.par], (u.turn + 1) * 32)
                wait(act, y_ps, upto(u, 2))
                a.copy(w2h[u.par][:, 0, :], raw2[u.par][:, 0, :])
                a.copy(w2h[u.par][0:FR, 1, :], raw2[u.par][0:FR, 1, :]).then_inc(w2h_s, 1)

            phase2(act, pairs, lambda s: units(s, (1, silu), (-1, w1_high), (1, h_high), (2, y_out), (-1, x_high), (0, w2_high)))

        @block.tensor
        def _(pe):
            pe.wait_ge(const_pool, 1)

            def turn_probs(b):
                pe.wait_ge(probs_sb, b.n + 1)
                wait(pe, pT_sb, b.n)
                for c in range(MK):
                    mm = pe.transpose(bank[2][0:MC, c * T:(c + 1) * T], pr[b.par][:, c * MC:(c + 1) * MC], ident[0:T, 0:T])
                mm.then_inc(pT_ps, 1)

            def turn_xn2(b):
                pe.wait_ge(xn2_s, b.n + 1)
                wait(pe, xn2T_sb, b.n)
                for c in range(DK):
                    mm = pe.transpose(bank[4][:, c * T:(c + 1) * T], xn2[b.par][:, c * P:(c + 1) * P], ident[0:T, 0:T])
                mm.then_inc(xn2T_ps, 1)

            def scores(b):
                pe.wait_ge(ctxT_in[b.par], (b.turn + 1) * 16)
                pe.wait_ge(xnT_sb, b.n + 1)
                wait(pe, c_score, b.n * SCORE)
                for c in range(DK):
                    mm = pe.matmul(bank[1][0:T, 0:M], xnT[b.par][:, c, :], ctxT_s[b.par][:, c, :],
                                   start=(c == 0), stop=(c == DK - 1))
                mm.then_inc(score_ps, 1)

            def readout(b):
                pe.wait_ge(ctx_in[b.par], (b.turn + 1) * 16)
                pe.wait_ge(pT_sb, b.n + 1)
                wait(pe, c_resid, b.n * RESID)
                for c in range(MK):
                    mm = pe.matmul(bank[3][0:T, :], pT[b.par][:, c, :], ctx_s[b.par][:, c, :],
                                   start=(c == 0), stop=(c == MK - 1))
                mm.then_inc(read_ps, 1)

            def logits(b):
                pe.wait_ge(xn2T_sb, b.n + 1)
                wait(pe, c_top, b.n * TOP)
                for c in range(DK):
                    mm = pe.matmul(bank[5][0:T, 0:E], xn2T[b.par][:, c, :], gw_s[:, c, :],
                                   start=(c == 0), stop=(c == DK - 1))
                mm.then_inc(logit_ps, 1)

            def places(b):
                pe.wait_ge(c_top, (b.n + 1) * TOP)
                wait(pe, c_place, b.n * PLACE)
                pe.matmul(bank[6][0:T, 0:E], ones_f[0:1, 0:T], list_base[0:1, :], start=True, stop=False)
                pe.matmul(bank[6][0:T, 0:E], tri[:], mk[b.par][:, 1, :], start=False, stop=False)
                mm = pe.matmul(bank[6][0:T, 0:E], minus[:], run[b.par][:, 1, :], start=False, stop=True)
                mm.then_inc(place_ps, 1)

            def spread(b):
                pe.wait_ge(c_place, (b.n + 1) * PLACE)
                wait(pe, c_slots, b.n * SLOTS)
                pe.matmul(bank[7][:, 0:ENTERS], ident[0:T, :], placed8[:, 0:ENTERS], start=True, stop=False)
                pe.matmul(bank[7][:, 0:ENTERS], spread_to[:], last8[:], start=False, stop=True).then_inc(spread_ps, 1)

            def turn_xn(b):
                pe.wait_ge(xn_s, b.n + 1)
                wait(pe, xnT_sb, b.n)
                for c in range(DK):
                    mm = pe.transpose(bank[0][:, c * T:(c + 1) * T], xn[b.par][:, c * P:(c + 1) * P], ident[0:T, 0:T])
                mm.then_inc(xnT_ps, 1)

            def slot(s):
                if isinstance(s.g, int) and s.off == 2:
                    pe.wait_ge(const_pool, CONSTS)
                    pe.wait_ge(const_in, 32)
                    pe.wait_ge(const_dve, DVE_CONSTS)
                stages(s)

            stages = (lambda s: batches(s, (1, turn_probs), (0, scores), (1, readout), (4, spread), (2, turn_xn2),
                                         (-1, turn_xn), (2, logits), (3, places)))
            phase1(pe, slot)

            pe.wait_ge(c_top, B * TOP)
            pe.matmul(bank[0][0:E, 0:E], ones_b[0:T, 0:E], run[0][:, 0, :], start=True, stop=True)
            pe.matmul(bank[0][0:E, 64:80], run[0][:, 0, :], ones_b[0:T, 0:16], start=True, stop=True)
            pe.matmul(bank[0][0:E, 80:96], run[0][:, 1, :], ones_b[0:T, 0:16], start=True, stop=True).then_inc(plan_ps, 1)
            pe.wait_ge(c_plan, PLAN_A)
            pe.matmul(bank[0][:, 128:192], nover_b[:], tri_incl[:], start=True, stop=True)
            pe.matmul(bank[0][:, 192:256], nover_b[:], ident_b[:], start=True, stop=True)
            pe.matmul(bank[0][:, 256:320], map_b[:], ident_b[:], start=True, stop=True).then_inc(plan_ps, 1)

            pairs = pairs_of(pe)

            def turn_rows(u):
                pe.wait_ge(gathered[u.par], (before_par(u) + tiles(u)) * 16)
                wait(pe, xh_s, before(u))
                wait(pe, xl_s, before(u))
                for t in range(tiles(u)):
                    for c in range(DK):
                        mm = pe.transpose(bank[6 + t][:, c * P:(c + 1) * P], xg[u.par][:, t, c * P:(c + 1) * P], ident[:])
                    mm.then_inc(xT_ps, 1)

            def gate_up(u):
                W = tiles(u) * P
                pe.wait_ge(w1l_s, u.n + 1)
                pe.wait_ge(xl_s, before(u) + tiles(u))
                wait(pe, h_s, (u.n - 1) * 3)
                if u.kind == "over":
                    o = bank[u.par][:, 0:2 * F]
                    for c in range(DK):
                        wh, wl, mh, ml = w1h[u.par][:, c, :], w1l[u.par][:, c, :], xh[u.par][:, c, 0:P], xl[u.par][:, c, 0:P]
                        pe.matmul(o, mh, wh, start=(c == 0), stop=False)
                        pe.matmul(o, mh, wl, start=False, stop=False)
                        mm = pe.matmul(o, ml, wh, start=False, stop=(c == DK - 1))
                    mm.then_inc(gu_ps, 1)
                    return
                for m in range(3):
                    o = (bank[u.par][:, m * UNIT:m * UNIT + W] if m < 2 else bank[2 + u.par][:, 0:W])
                    for c in range(DK):
                        wh, wl = w1h[u.par][:, c, m * P:(m + 1) * P], w1l[u.par][:, c, m * P:(m + 1) * P]
                        mh, ml = xh[u.par][:, c, 0:W], xl[u.par][:, c, 0:W]
                        pe.matmul(o, wh, mh, start=(c == 0), stop=False)
                        pe.matmul(o, wh, ml, start=False, stop=False)
                        mm = pe.matmul(o, wl, mh, start=False, stop=(c == DK - 1))
                mm.then_inc(gu_ps, 1)

            def turn_h(u):
                pe.wait_ge(h_s, (u.n + 1) * 3)
                wait(pe, hl_s, u.n - 1)
                for k in range(2):
                    mm = pe.transpose(bank[2 + u.par][:, k * P:(k + 1) * P], h[:, 0, k * P:(k + 1) * P], ident[:])
                mm.then_inc(hT_ps, 1)

            def down(u):
                pe.wait_ge(hl_s, u.n + 1)
                pe.wait_ge(w2l_s, u.n + 1)
                wait(pe, ys_s, before(u))
                for t in range(tiles(u)):
                    s = slice(t * P, (t + 1) * P)
                    o = bank[4 + t][:]
                    pe.matmul(o, hh[u.par][:, 0, s], w2h[u.par][:, 0, :], start=True, stop=False)
                    pe.matmul(o, hh[u.par][:, 0, s], w2l[u.par][:], start=False, stop=False)
                    pe.matmul(o, hl[u.par][:, 0, s], w2h[u.par][:, 0, :], start=False, stop=False)
                    pe.matmul(o, hh[u.par][:, 1, s], w2h[u.par][:, 1, :], start=False, stop=False)
                    pe.matmul(o, hl[u.par][0:FR, 1, s], w2h[u.par][0:FR, 1, :], start=False, stop=True).then_inc(y_ps, 1)

            phase2(pe, pairs, lambda s: units(s, (-1, turn_rows), (1, only("over", turn_h)), (0, gate_up), (1, down)))


DVE_CONSTS = 7
CONSTS = 18 + 3 * NSENT

PLAN_A, PLAN = 1, 2


def kernel(x, ctx_2048, mask_BxS2_bk0, L0_ffn_gate_weight, L0_ffn_gate_up_proj, L0_ffn_down_proj, L0_ffn_similarity):
    import numpy as np
    import concourse.bacc as bacc
    from concourse.bass_utils import run_bass_kernel_spmd

    ctx = np.asarray(ctx_2048)
    ctxT = ctx.transpose(0, 2, 1).reshape(B, DK, P, M).transpose(0, 2, 1, 3)
    gwT = np.asarray(L0_ffn_gate_weight).T.reshape(DK, P, E).transpose(1, 0, 2)
    gu = np.asarray(L0_ffn_gate_up_proj)
    gate, up = gu[:, :F], gu[:, F:]
    w1 = np.concatenate([gate[:, :P], up[:, :P], gate[:, P:], up[:, P:]], axis=1)
    w1 = w1.transpose(0, 2, 1).reshape(E, DK, P, 2 * F).transpose(0, 2, 1, 3).reshape(E, P, DK * 2 * F)
    w2 = np.asarray(L0_ffn_down_proj).transpose(0, 2, 1)
    data = {
        "in_x": np.asarray(x), "in_ctx": ctx, "in_ctxT": ctxT,
        "in_mask": np.asarray(mask_BxS2_bk0), "in_gwT": gwT, "in_w1": w1,
        "in_w2a": w2[:, :P], "in_w2b": w2[:, P:], "in_sim": np.asarray(L0_ffn_similarity),
    }
    data = {k: np.ascontiguousarray(a) for k, a in data.items()}
    nc = bacc.Bacc("TRN2", target_bir_lowering=False, num_devices=1)
    args = [nc.dram_tensor(k, a.shape, mybir.dt.from_np(a.dtype), kind="ExternalInput").ap() for k, a in data.items()]
    args.append(nc.dram_tensor("out_rows", (ROWS, D), F32, kind="ExternalOutput").ap())
    program(nc, *args)
    rows = run_bass_kernel_spmd(nc, [data], core_ids=[0]).results[0]["out_rows"]
    return rows[:TOK].reshape(B, T, D)
```
